# Optimizing a Trainium2 kernel written in Bass

```python
import numpy as np
import jax
import jax.numpy as jnp

def _softmax(x, axis=-1):
    return jax.nn.softmax(x, axis=axis)
def _gelu(x):
    return jax.nn.gelu(x, approximate=True)
def _silu(x):
    return jax.nn.silu(x)
def _sigmoid(x):
    return jax.nn.sigmoid(x)
def _layernorm(x, axis=-1, eps=1e-5):
    m = jnp.mean(x, axis=axis, keepdims=True)
    v = jnp.var(x, axis=axis, keepdims=True)
    return (x - m) / jnp.sqrt(v + eps)
def _scatter_add(tgt, idx, src, axis=0):
    return tgt.at[idx].add(src)
def _segment_sum(src, seg, n):
    return jax.ops.segment_sum(src, seg, n)

kernel_name = 'mk_adj_preln_d1_adj_128_044989'

def setup_inputs(seed: int = 0):
    np.random.seed(seed)
    _w = jnp.asarray
    def _rec_inputs():
        import jax
        import jax.numpy as jnp
        _gk = jax.random.key(seed)
        x = -0.003407 + 1.001 * jax.random.normal(jax.random.fold_in(_gk, 1), (3327, 128), jnp.float32)
        _a = jax.random.bernoulli(jax.random.fold_in(_gk, 2), 0.00240457, (3327, 3327))
        _a = jnp.logical_or(_a, jnp.swapaxes(_a, -1, -2))
        _a = jnp.logical_or(_a, jnp.eye(3327, dtype=bool))
        _af = _a.astype(jnp.float32)
        _af = _af * jax.random.uniform(jax.random.fold_in(_gk, 3), (3327, 3327), jnp.float32, 0.05, 5.06092)
        adj = _af
        return x, adj
    x, adj = _rec_inputs()
    def _L0_gnn_setup():
        import jax, jax.numpy as jnp
        import numpy as np
        N = 1024
        D = 128
        H = 8
        key = jax.random.key(seed)
        ks = jax.random.split(key, 7)
        s = (D * H) ** (-0.5)
        return {'x': jax.random.normal(ks[0], (N, D), dtype=jnp.float32), 'spatial_encoding': jax.random.normal(ks[1], (N, N), dtype=jnp.float32), 'edge_encoding': jax.random.normal(ks[2], (N, N), dtype=jnp.float32), 'Wq': jax.random.normal(ks[3], (D * H, D), dtype=jnp.float32) * s, 'Wk': jax.random.normal(ks[4], (D * H, D), dtype=jnp.float32) * s, 'Wv': jax.random.normal(ks[5], (D * H, D), dtype=jnp.float32) * s, 'Wo': jax.random.normal(ks[6], (D, D * H), dtype=jnp.float32) * s}
    _L0_gnn_all = _L0_gnn_setup()
    _L0_gnn_in = {k: v for k, v in _L0_gnn_all.items() if k in ('Wq', 'Wk', 'Wv', 'Wo', )}
    del _L0_gnn_all

    return {
        "x": x,
        "adj": adj,
        "L0_gnn_Wq": _L0_gnn_in["Wq"],
        "L0_gnn_Wk": _L0_gnn_in["Wk"],
        "L0_gnn_Wv": _L0_gnn_in["Wv"],
        "L0_gnn_Wo": _L0_gnn_in["Wo"],
    }

def reference(x, adj, L0_gnn_Wq, L0_gnn_Wk, L0_gnn_Wv, L0_gnn_Wo):
    import jax
    import jax.numpy as jnp
    def _L0_gnn_ref(x, spatial_encoding, edge_encoding, Wq, Wk, Wv, Wo):
        import jax, jax.numpy as jnp
        import numpy as np
        N = 1024
        D = 128
        H = 8
        n, d = x.shape
        h = Wq.shape[0] // d
        scale = d ** (-0.5)
        q = (x @ Wq.T).reshape(d, n, h)
        k = (x @ Wk.T).reshape(d, n, h)
        v = (x @ Wv.T).reshape(d, n, h)
        a = jnp.einsum('dnh,dmh->dnm', q, k) * scale
        a = a + spatial_encoding + edge_encoding
        a = jax.nn.softmax(a, axis=2)
        out = jnp.einsum('dnm,dmh->dnh', a, v)
        out = out.reshape(n, h * d)
        return out @ Wo.T

    h = jnp.maximum(_layernorm(x, axis=-1), 0.0)
    x = x + _L0_gnn_ref(h, adj, adj, L0_gnn_Wq, L0_gnn_Wk, L0_gnn_Wv, L0_gnn_Wo)
    return x


_drawn_inputs = setup_inputs


def setup_inputs(seed=0):
    import zlib

    import numpy as np

    out = dict(_drawn_inputs(seed))
    spreads = {}
    factors = {'L0_gnn_Wq': 8.0, 'L0_gnn_Wk': 8.0}
    for name, (base, spread) in spreads.items():
        noise = np.random.default_rng([zlib.crc32(name.encode()), seed]).standard_normal(out[name].shape)
        drawn = base * np.exp(spread * noise) if base else spread * noise
        out[name] = jnp.asarray(drawn.astype(out[name].dtype))
    for name, factor in factors.items():
        out[name] = (out[name] * factor).astype(out[name].dtype)
    return out
```

```python
from contextlib import ExitStack

import concourse.bass as bass
from concourse import mybir

N = 3327
D = 128
H = 8
P = 128
NT = (N + P - 1) // P
NPAD = NT * P
LAST = N - (NT - 1) * P
FLAT = NPAD * P
PARTS = 4
STEP = N // PARTS
W = N - (PARTS - 1) * STEP
RT = (W + P - 1) // P
RLAST = W - (RT - 1) * P
CH = 4
CHS = [W * c // CH for c in range(CH + 1)]
CHW = max(CHS[c + 1] - CHS[c] for c in range(CH))
VC = H + 1
SPLIT = 3
KR = SPLIT + SPLIT * SPLIT * H
SCALE = float(D) ** -0.5
EPS = 1e-5
MASKED = -1.0e30
SAFE = 34.0
BANK = 512
SLOTS = 3
START = 1
VROW = (NPAD + 1) * VC
ARENA = 240 * P
GROUPS = [(4 * k, min(4, NT - 4 * k)) for k in range((NT + 3) // 4)]
SEGS = [(a, min(BANK, W - a)) for a in range(0, W, BANK)]

fp32 = mybir.dt.float32
bf16 = mybir.dt.bfloat16
i32 = mybir.dt.int32
ALU = mybir.AluOpType
ACT = mybir.ActivationFunctionType
AX = mybir.AxisListType


def build(nc, x, adj, wq, wk, wv, wo, out):
    qk_d = nc.dram_tensor("qk_pieces", [SPLIT, 2, H, FLAT], bf16).ap()
    shift_d = nc.dram_tensor("shift_pieces", [SPLIT, FLAT], bf16).ap()
    qnorm_d = nc.dram_tensor("qnorm", [FLAT], fp32).ap()
    v_d = nc.dram_tensor("values", [2 * P, VROW], fp32).ap()
    o_d = nc.dram_tensor("attended", [VC, FLAT], fp32).ap()

    ctx = ExitStack()
    with ctx:
        def sb(name, shape, dt=fp32):
            return ctx.enter_context(nc.sbuf_tensor(name, shape, dt))

        def sem(name):
            return ctx.enter_context(nc.semaphore(name))

        arena = sb("arena", [P, ARENA])
        bias = arena[:, 0:NT * W].rearrange("p (t n) -> p t n", n=W)
        room = arena[:, :]
        used = [0]

        def carve(cols, dt=fp32):
            a = used[0]
            used[0] = a + cols
            v = room[:, a:a + cols]
            return v if dt == fp32 else v.bitcast(dt)

        nat = [sb(f"nat{b}", [P, N]) for b in range(2)]
        keys = [sb(f"keys{b}", [KR, NPAD], bf16) for b in range(2)]
        queries = [sb(f"queries{b}", [KR, W], bf16) for b in range(2)]
        values = [sb(f"values{b}", [P, NT * VC]) for b in range(2)]
        XD, XG = 5, 3
        slots = [arena[:, (NT + b) * W:(NT + b + 1) * W] for b in range(XD + XG)]
        xd, xg = slots[:XD], slots[XD:]
        attended = [sb(f"attended_sb{b}", [P, CHW]) for b in range(2)]
        ident = sb("ident", [P, P])
        small = sb("small", [P, 512])
        flag = sb("flag", [P, 1], i32)

        scores = ctx.enter_context(nc.psum_tensor("scores", [P, SLOTS, 2 * BANK], fp32))
        acc = ctx.enter_context(nc.psum_tensor("acc", [P, 2, BANK], fp32))
        banks = scores[:, :, :].rearrange("p a (b n) -> p (a b) n", n=BANK)
        flatp = scores[:, :, :].rearrange("p a n -> p (a n)")

        prepare(nc, ctx, sem, carve, x, wq, wk, wv, qk_d, qnorm_d, v_d, o_d, shift_d, nat, keys, ident, small, flag,
                banks, flatp, acc)
        attend(nc, sem, adj, qk_d, shift_d, v_d, o_d, bias, nat, keys, queries, values, xd, xg, attended, ident,
               small, flag, scores, banks, flatp, acc)
        used[0] = 0
        project(nc, sem, carve, x, wo, o_d, out, ident, banks, flatp, acc)


def prepare(nc, ctx, sem, carve, x, wq, wk, wv, qk_d, qnorm_d, v_d, o_d, shift_d, nat, keys, ident, small, flag,
            banks, flatp, acc):
    x_all = carve(NT * P).rearrange("p (t c) -> p t c", c=P)
    sq_all = carve(NT * P).rearrange("p (t c) -> p t c", c=P)
    w_raw = [carve(H * P).rearrange("p (h c) -> p h c", c=P) for _ in range(3)]
    w_t = [carve(H * P).rearrange("p (h g) -> p h g", g=P) for _ in range(3)]
    h_row = [carve(P) for _ in range(2)]
    h_t = [carve(P) for _ in range(2)]
    pieces = [carve(SPLIT * 2 * H * P // 2, bf16).rearrange("p (s m n) -> p s m n", s=SPLIT, m=2) for _ in range(2)]
    rest = [carve(H * P) for _ in range(4)]
    square = [carve(H * P) for _ in range(2)]
    v_out = [carve(P * VC).rearrange("p (r h) -> p r h", h=VC) for _ in range(2)]
    norm = [carve(2 * P).rearrange("p (m g) -> p m g", m=2) for _ in range(2)]
    top = carve(2 * P).rearrange("p (m g) -> p m g", m=2)

    mean, var, root, inv = (small[:, 32 * i:32 * i + NT] for i in range(4))
    half = small[:, 128:128 + NT]
    peak, peaks, bound, safe, keep, negkeep = (small[:, 160 + 2 * i:162 + 2 * i] for i in range(6))

    x_padded, x_loaded, w_loaded = sem("x_padded"), sem("x_loaded"), sem("w_loaded")
    zeroed, ident_ready, w_turned, w_ready = sem("zeroed"), sem("ident_ready"), sem("w_turned"), sem("w_ready")
    chain, var_ready, root_ready, ln_done = sem("chain"), sem("var_ready"), sem("root_ready"), sem("ln_done")
    h_ready, h_turned, h_t_ready = sem("h_ready"), sem("h_turned"), sem("h_t_ready")
    projected = [sem("q_projected"), sem("k_projected"), sem("v_projected")]
    first_piece = [sem("q_first"), sem("k_first")]
    squared = [sem("q_squared"), sem("k_squared")]
    rest_ready = [sem("q_rest"), sem("k_rest")]
    normed = [sem("q_normed"), sem("k_normed")]
    second_piece = [sem("q_second"), sem("k_second")]
    third_piece = [sem("q_third"), sem("k_third")]
    v_ready, norm_kept = sem("v_ready"), sem("norm_kept")
    stored = [sem("pieces_stored0"), sem("pieces_stored1")]
    v_stored = [sem("v_stored0"), sem("v_stored1")]
    peak_ready, peaks_ready, safe_ready = sem("peak_ready"), sem("peaks_ready"), sem("safe_ready")
    norms_loaded, clamped, shift_root = sem("norms_loaded"), sem("clamped"), sem("shift_root")
    shift_ready, shift_stored, pad_stored = sem("shift_ready"), sem("shift_stored"), sem("pad_stored")
    seconds_ready = sem("seconds_ready")

    shift = nat[0]
    shift_rest = nat[1]

    qk_rows = qk_d.rearrange("s m h (r g) -> r (s m h) g", g=P)
    norm_rows = qnorm_d.rearrange("(r g) -> r g", g=P)
    sp_pieces = sq_all.rearrange("p t c -> p (t c)")
    x_pieces = x_all.rearrange("p t c -> p (t c)")
    piece_a = sp_pieces.bitcast(bf16)[:, 0:N]
    piece_b = sp_pieces.bitcast(bf16)[:, NPAD:NPAD + N]
    piece_c = x_pieces.bitcast(bf16)[:, 0:N]

    with nc.Block() as block:
        @block.sync
        def _(sp):
            for s in (h_t_ready, h_turned, v_ready, projected[2], *squared, *rest_ready, *normed, *second_piece, *third_piece,
                      *stored, *v_stored):
                sp.sem_inc(s, START)
            sp.dma_start(x_all[:, 0:NT - 1, :],
                         x[0:(NT - 1) * P, :].rearrange("(t p) c -> p t c", p=P)).then_inc(x_loaded, 16)
            sp.wait_ge(x_padded, 1)
            sp.dma_start(x_all[0:LAST, NT - 1, :], x[(NT - 1) * P:N, :]).then_inc(x_loaded, 16)
            for m, w in enumerate((wq, wk, wv)):
                sp.dma_start(w_raw[m], w.rearrange("(g h) c -> g h c", h=H)).then_inc(w_loaded, 16)
            with sp.Fori(0, NT // 2) as pair:
                for b in range(2):
                    i = pair * 2 + b
                    for m in range(2):
                        sp.wait_ge(second_piece[m], i + 1 + START)
                        sp.wait_ge(third_piece[m], i + 1 + START)
                    sp.wait_ge(normed[0], i + 1 + START)
                    sp.dma_start(qk_rows[bass.ds(i * P, P), :, :],
                                 pieces[b].rearrange("p s m (h g) -> p (s m h) g", g=P)).then_inc(stored[b], 16)
                    sp.dma_start(norm_rows[bass.ds(i * P, P), :], norm[b][:, 0, :]).then_inc(stored[b], 16)
                    sp.wait_ge(v_ready, i + 1 + START)
                    sp.dma_start(v_d[P:2 * P, bass.ds(i * (P * VC), P * VC)],
                                 v_out[b].rearrange("p r h -> p (r h)")).then_inc(v_stored[b], 16)
                    sp.dma_start(v_d[0:P, bass.ds(i * (P * VC) + VC, P * VC)],
                                 v_out[b].rearrange("p r h -> p (r h)")).then_inc(v_stored[b], 16)
            sp.wait_ge(zeroed, 1)
            sp.dma_start(o_d[:, N * P:FLAT], small[0:VC, 256:256 + P]).then_inc(pad_stored, 16)
            for b in range(2):
                sp.wait_ge(stored[b], 32 * (NT // 2) + START)
                sp.wait_ge(v_stored[b], 32 * (NT // 2) + START)
            sp.dma_start(shift[:, :], qnorm_d[0:N * D].rearrange("(d n) -> d n", n=N)).then_inc(norms_loaded, 16)
            sp.wait_ge(shift_ready, 1)
            sp.wait_ge(seconds_ready, 1)
            for s, piece in enumerate((piece_a, piece_b, piece_c)):
                sp.dma_start(shift_d[s, 0:N * D].rearrange("(d n) -> d n", n=N), piece).then_inc(shift_stored, 16)
            sp.dma_start(shift_d[:, N * D:FLAT], small[0:SPLIT, 384:384 + P // 2].bitcast(bf16)).then_inc(shift_stored, 16)
            sp.wait_ge(shift_stored, 64)
            sp.wait_ge(pad_stored, 16)

        @block.gpsimd
        def _(pool):
            nc.gpsimd.memset(small[:, 256:512], 0.0).then_inc(zeroed, 1)
            nc.gpsimd.memset(ident[:, :], 0.0).then_inc(ident_ready, 1)
            pool.wait_ge(ident_ready, 1)
            nc.gpsimd.affine_select(out=ident[:, :], in_=ident[:, :], compare_op=ALU.not_equal, fill=1.0, base=0,
                                    pattern=[[-1, P]], channel_multiplier=1).then_inc(ident_ready, 1)
            with pool.Fori(0, NT // 2) as pair:
                for b in range(2):
                    i = pair * 2 + b
                    for m in range(2):
                        pool.wait_ge(second_piece[m], i + 1 + START)
                        nc.gpsimd.tensor_tensor(pieces[b][:, 2, m, :], rest[2 * b + m], pieces[b][:, 1, m, :],
                                                ALU.subtract).then_inc(third_piece[m], 1)
            pool.wait_ge(peak_ready, 1)
            nc.gpsimd.partition_all_reduce(peaks, peak, P, bass.bass_isa.ReduceOp.max).then_inc(peaks_ready, 1)

        @block.tensor
        def _(pe):
            pe.wait_ge(ident_ready, 2)
            pe.wait_ge(w_loaded, 48)
            for m in range(3):
                for h in range(H):
                    last = nc.tensor.transpose(banks[:, 2 * m + h // 4, P * (h % 4):P * (h % 4 + 1)],
                                               w_raw[m][:, h, :], ident[:, :])
                last.then_inc(w_turned, 1)
            with pe.Fori(0, NT // 2) as pair:
                for b in range(2):
                    i = pair * 2 + b
                    pe.wait_ge(h_ready, i + 1)
                    pe.wait_ge(h_t_ready, i + START)
                    nc.tensor.transpose(acc[:, 0, 0:P], h_row[b], ident[:, :]).then_inc(h_turned, 1)
                    pe.wait_ge(h_t_ready, i + 1 + START)
                    if b == 0:
                        pe.wait_ge(w_ready, 3)
                    for m in range(2):
                        pe.wait_ge(squared[m], i + START)
                        pe.wait_ge(rest_ready[m], i + START)
                        for s in range(2):
                            last = nc.tensor.matmul(banks[:, 2 * m + s, :], h_t[b],
                                                    w_t[m][:, 4 * s:4 * s + 4, :].rearrange("p h g -> p (h g)"),
                                                    start=True, stop=True)
                        last.then_inc(projected[m], 1)
                    pe.wait_ge(v_ready, i + START)
                    for h in range(H):
                        last = nc.tensor.matmul(banks[:, 4 + h // 4, P * (h % 4):P * (h % 4 + 1)], w_t[2][:, h, :],
                                                h_t[b], start=True, stop=True)
                    last.then_inc(projected[2], 1)

        @block.scalar
        def _(act):
            act.wait_ge(var_ready, 1)
            nc.scalar.activation(root, var, ACT.Sqrt).then_inc(root_ready, 1)
            for m in range(3):
                act.wait_ge(w_turned, m + 1)
                nc.scalar.copy(w_t[m].rearrange("p h g -> p (h g)"),
                               flatp[:, 2 * m * BANK:2 * (m + 1) * BANK]).then_inc(w_ready, 1)
            with act.Fori(0, NT // 2) as pair:
                for b in range(2):
                    i = pair * 2 + b
                    act.wait_ge(h_turned, i + 1 + START)
                    act.wait_ge(projected[2], pair * 2 + START)
                    nc.scalar.copy(h_t[b], acc[:, 0, 0:P]).then_inc(h_t_ready, 1)
                    act.wait_ge(stored[b], pair * 32 + START)
                    for m in range(2):
                        src = flatp[:, 2 * m * BANK:2 * (m + 1) * BANK]
                        scale = SCALE if m == 0 else 1.0
                        act.wait_ge(projected[m], i + 1)
                        nc.scalar.activation(pieces[b][:, 0, m, :], src, ACT.Copy, scale=scale).then_inc(first_piece[m], 1)
                        act.wait_ge(normed[m], i + START)
                        nc.scalar.activation(square[m], src, ACT.Square, scale=scale).then_inc(squared[m], 1)
                    for m in range(2):
                        act.wait_ge(rest_ready[m], i + 1 + START)
                        nc.scalar.copy(pieces[b][:, 1, m, :], rest[2 * b + m]).then_inc(second_piece[m], 1)
            act.wait_ge(clamped, 1)
            nc.scalar.activation(shift[:, :], shift[:, :], ACT.Sqrt).then_inc(shift_root, 1)
            act.wait_ge(shift_ready, 1)

        @block.vector
        def _(dve):
            links = [0]

            def link(ins):
                links[0] += 1
                ins.then_inc(chain, 1)
                dve.wait_ge(chain, links[0])

            nc.vector.memset(x_all[:, NT - 1, :], 0.0).then_inc(x_padded, 1)
            nc.vector.memset(top, 0.0)
            for b in range(2):
                nc.vector.memset(v_out[b], 1.0)
            link(nc.vector.memset(acc[:, :, :], 0.0))
            dve.wait_ge(x_loaded, 32)
            link(nc.vector.reduce_sum(mean, x_all, axis=AX.X))
            link(nc.vector.tensor_scalar(mean, mean, 1.0 / D, None, ALU.mult))
            link(nc.vector.tensor_tensor(x_all, x_all, mean.unsqueeze(2).to_broadcast([P, NT, P]), ALU.subtract))
            link(nc.vector.tensor_tensor(sq_all, x_all, x_all, ALU.mult))
            link(nc.vector.reduce_sum(var, sq_all, axis=AX.X))
            nc.vector.tensor_scalar(var, var, 1.0 / D, EPS, ALU.mult, ALU.add).then_inc(var_ready, 1)
            dve.wait_ge(var_ready, 1)
            dve.wait_ge(root_ready, 1)
            link(nc.vector.reciprocal(inv, root))
            link(nc.vector.tensor_tensor(half, var, inv, ALU.mult))
            link(nc.vector.tensor_tensor(half, half, root, ALU.add))
            link(nc.vector.tensor_scalar(half, half, 0.5, None, ALU.mult))
            link(nc.vector.reciprocal(inv, half))
            link(nc.vector.tensor_tensor(x_all, x_all, inv.unsqueeze(2).to_broadcast([P, NT, P]), ALU.mult))
            with dve.Fori(0, NT // 2) as pair:
                for b in range(2):
                    i = pair * 2 + b
                    dve.wait_ge(h_turned, pair * 2 + START)
                    nc.vector.tensor_scalar(h_row[b], x_all[:, bass.ds(i, 1), :].rearrange("p o c -> p (o c)"), 0.0,
                                            None, ALU.max).then_inc(h_ready, 1)
                    for m in range(2):
                        src = flatp[:, 2 * m * BANK:2 * (m + 1) * BANK]
                        dve.wait_ge(first_piece[m], i + 1)
                        dve.wait_ge(third_piece[m], pair * 2 + START)
                        dve.wait_ge(squared[m], i + 1 + START)
                        nc.vector.scalar_tensor_tensor(rest[2 * b + m], src, SCALE if m == 0 else 1.0,
                                                       pieces[b][:, 0, m, :], ALU.mult,
                                                       ALU.subtract).then_inc(rest_ready[m], 1)
                        dve.wait_ge(stored[b], pair * 32 + START)
                        nc.vector.reduce_sum(norm[b][:, m, :], square[m].rearrange("p (h g) -> p g h", g=P),
                                             axis=AX.X).then_inc(normed[m], 1)
                    dve.wait_ge(projected[2], i + 1 + START)
                    dve.wait_ge(v_stored[b], pair * 32 + START)
                    nc.vector.tensor_copy(v_out[b][:, :, 0:H],
                                          flatp[:, 4 * BANK:6 * BANK].rearrange("p (h r) -> p r h", r=P)).then_inc(v_ready, 1)
                    dve.wait_ge(normed[1], i + 1 + START)
                    nc.vector.tensor_tensor(top, top, norm[b], ALU.max).then_inc(norm_kept, 1)
                    dve.wait_ge(norm_kept, i + 1)
            link(nc.vector.tensor_reduce(peak, top, AX.X, ALU.max))
            nc.vector.tensor_copy(peak, peak).then_inc(peak_ready, 1)
            dve.wait_ge(peaks_ready, 1)
            link(nc.vector.tensor_tensor(bound[:, 0:1], peaks[:, 0:1], peaks[:, 1:2], ALU.mult))
            link(nc.vector.tensor_scalar(keep[:, 0:1], bound[:, 0:1], SAFE * SAFE, None, ALU.is_le))
            nc.vector.tensor_copy(flag[:, :], keep[:, 0:1])
            link(nc.vector.tensor_scalar(negkeep[:, 0:1], keep[:, 0:1], -1.0, None, ALU.mult))
            dve.wait_ge(norms_loaded, 16)
            nc.vector.tensor_scalar(shift[:, :], shift[:, :], peaks[:, 1:2], 1e-30, ALU.mult, ALU.max).then_inc(clamped, 1)
            dve.wait_ge(shift_root, 1)
            link(nc.vector.tensor_scalar(shift[:, :], shift[:, :], negkeep[:, 0:1], None, ALU.mult))
            link(nc.vector.tensor_copy(piece_a, shift[:, :]))
            link(nc.vector.tensor_tensor(shift_rest[:, :], shift[:, :], piece_a, ALU.subtract))
            nc.vector.tensor_copy(piece_b, shift_rest[:, :]).then_inc(seconds_ready, 1)
            dve.wait_ge(seconds_ready, 1)
            nc.vector.tensor_tensor(piece_c, shift_rest[:, :], piece_b, ALU.subtract).then_inc(shift_ready, 1)


class Path:

    def __init__(self, name, factored):
        self.name = name
        self.factored = factored
        self.kind = ["g" if factored and t % 4 == 3 else "d" for t in range(NT)]
        self.nd, self.ng = self.kind.count("d"), self.kind.count("g")
        self.order = sorted(range(NT), key=lambda t: t + (2 if self.kind[t] == "g" else 0))

        self.exp_order = sorted(range(NT), key=lambda t: t - (1.5 if self.kind[t] == "g" else 0))

    def exped_with(self, t):
        return self.exp_order.index(t) + 1

    def weighed_since(self, n, kind, slots):
        tiles = [t for t in range(NT) if self.kind[t] == kind]
        holder = tiles[n - slots]
        return self.order.index(holder) + 1 - (NT if n < slots else 0)

    def before(self, t, kind):
        return self.kind[:t].count(kind)


def attend(nc, sem, adj, qk_d, shift_d, v_d, o_d, bias, nat, keys, queries, values, xd, xg, attended, ident, small,
           flag, scores, banks, flatp, acc):
    fast, general = Path("fast", True), Path("general", False)
    args = (adj, qk_d, shift_d, v_d, o_d, bias, nat, keys, queries, values, xd, xg, attended, ident, small, scores,
            banks, flatp, acc)
    programs = [attention_programs(nc, sem, path, *args) for path in (fast, general)]
    ready = sem("attention_constants")

    with nc.Block() as block:
        def either(engine, which):
            bounded = engine.value_load(flag[0:1, 0:1], min_val=0, max_val=1)
            with engine.If(bounded == 1):
                programs[0][which](engine)
            with engine.Else():
                programs[1][which](engine)

        @block.sync
        def _(sp):
            sp.wait_ge(ready, 1)
            either(sp, "sync")

        @block.gpsimd
        def _(pool):
            pool.wait_ge(ready, 1)
            either(pool, "gpsimd")

        @block.tensor
        def _(pe):
            pe.wait_ge(ready, 1)
            either(pe, "tensor")

        @block.scalar
        def _(act):
            act.wait_ge(ready, 1)
            either(act, "scalar")

        @block.vector
        def _(dve):
            for b in range(2):
                nc.vector.memset(keys[b][0:SPLIT, :], 1.0)
            nc.vector.memset(bias[96:P, NT - 1, :], MASKED)
            nc.vector.memset(acc[:, :, :], 0.0).then_inc(ready, 1)
            dve.wait_ge(ready, 1)
            either(dve, "vector")


def attention_programs(nc, sem, path, adj, qk_d, shift_d, v_d, o_d, bias, nat, keys, queries, values, xd, xg,
                       attended, ident, small, scores, banks, flatp, acc):
    name = path.name
    XD = max(n for n in range(1, len(xd) + 1) if 2 * path.nd % n == 0)
    XG = len(xg)
    nd, ng = path.nd, path.ng

    nat_loaded = [sem(f"{name}_nat_loaded{b}") for b in range(2)]
    row_max, nat_ready, nat_exp = sem(f"{name}_row_max"), sem(f"{name}_nat_ready"), sem(f"{name}_nat_exp")
    turned, even_copied, odd_copied = sem(f"{name}_turned"), sem(f"{name}_even_copied"), sem(f"{name}_odd_copied")
    qk_loaded = [sem(f"{name}_qk_loaded{b}") for b in range(2)]
    v_loaded = [sem(f"{name}_v_loaded{b}") for b in range(2)]
    scored = sem(f"{name}_scored")
    biased = sem(f"{name}_biased")
    exped = sem(f"{name}_exped")
    factored = sem(f"{name}_factored")
    weighed = sem(f"{name}_weighed")
    acc_free = [sem(f"{name}_acc_free{b}") for b in range(2)]
    out_stored = [sem(f"{name}_out_stored{b}") for b in range(2)]
    CREDIT = NT + START
    HALF = D // 2

    gview = lambda rows, b: nat[b][0:rows, 0:24 * P].rearrange("p (a q c) -> p a q c", q=4, c=P)[:, :, 3, :]
    rows_of = [P] * (RT - 1) + [RLAST]
    loads_of = [(RT + 1) // 2, RT // 2]

    def natural_count(part, j):
        return part * loads_of[j % 2] + j // 2 + 1

    def load_adjacency(sp, part):
        for j in range(RT):
            if j < 2:
                sp.wait_ge(turned, part * (RT * len(GROUPS)) + START)
            else:
                sp.wait_ge(turned, part * (RT * len(GROUPS)) + (j - 1) * len(GROUPS) + START)
            sp.dma_start(nat[j % 2][0:rows_of[j], :],
                         adj[bass.ds(part * STEP + j * P, rows_of[j]), :]).then_inc(nat_loaded[j % 2], 16)

    def load_batch(sp, d, part, b, loaded, shifted=True):
        for s in range(SPLIT):
            r = SPLIT + s * SPLIT * H
            sp.dma_start(keys[b][r:r + SPLIT * H, :], qk_d[:, 1, :, bass.ds(d * N, NPAD)]).then_inc(loaded, 16)
            sp.dma_start(queries[b][r:r + SPLIT * H, :],
                         qk_d[s, 0, :, bass.ds(d * N + part * STEP, W)].unsqueeze(0).to_broadcast([SPLIT, H, W])
                         ).then_inc(loaded, 16)
        if shifted:
            sp.dma_start(queries[b][0:SPLIT, :], shift_d[:, bass.ds(d * N + part * STEP, W)]).then_inc(loaded, 16)

    BATCH_DMAS = 2 * SPLIT + 1

    def sync(sp):
        for s, credit in ((scored, CREDIT), (weighed, CREDIT)):
            sp.sem_inc(s, credit)
        for s in (*acc_free, *out_stored, turned, even_copied, odd_copied, biased, factored):
            sp.sem_inc(s, START)
        if not path.factored:
            for s in (m_scored, m_added, m_run, m_stored):
                sp.sem_inc(s, START)
        with sp.Fori(0, PARTS) as part:
            load_adjacency(sp, part)
            if not path.factored:
                find_maxima_sync(sp, part)

            def load(pair, b):
                d = pair * 2 + b
                done = (part * D + d) * NT
                sp.wait_ge(scored, done - NT + CREDIT)
                sp.wait_ge(weighed, done - NT + CREDIT)
                load_batch(sp, d, part, b, qk_loaded[b])
                first = P * VROW - d * (VROW - NT * VC)
                sp.dma_start(values[b][:, :], value_band(v_d, first)).then_inc(v_loaded[b], 16)

            def store(pair, b):
                d = pair * 2 + b
                sp.wait_ge(acc_free[b], part * HALF + pair + 2)
                for c in range(CH):
                    w = CHS[c + 1] - CHS[c]
                    sp.dma_start(o_d[:, bass.ds(d * N + part * STEP + CHS[c], w)],
                                 attended[b][32 * c:32 * c + VC, 0:w]).then_inc(out_stored[b], 16)

            for b in range(2):
                load(0, b)
            with sp.Fori(1, HALF) as pair:
                for b in range(2):
                    load(pair, b)
                    store(pair - 1, b)
            for b in range(2):
                store(HALF - 1, b)
        for b in range(2):
            sp.wait_ge(out_stored[b], 16 * CH * HALF * PARTS + START)

    def tensor(pe):
        with pe.Fori(0, PARTS) as part:
            pe.wait_ge(biased, part * (nd * D) + START)
            for b in range(2):
                pe.wait_ge(acc_free[b], part * HALF + 1)
            for j in range(RT):
                rows = rows_of[j]
                tile = part * RT + j
                if path.factored:
                    pe.wait_ge(nat_exp, tile + 1)
                pe.wait_ge(nat_ready, tile + 1)
                for k, (t0, n) in enumerate(GROUPS):
                    if k % 2 == 0:
                        pe.wait_ge(even_copied, tile * 4 + (1 if k == 6 else 0) + START)
                    else:
                        pe.wait_ge(odd_copied, tile * 3 + START)
                    for t in range(t0, t0 + n):
                        cols = min(P, N - t * P)
                        last = nc.tensor.transpose(banks[0:cols, k % 6, P * (t - t0):P * (t - t0) + rows],
                                                   nat[j % 2][0:rows, t * P:t * P + cols], ident[0:rows, 0:rows])
                    last.then_inc(turned, 1)
            if not path.factored:
                find_maxima_tensor(pe, part)
            pe.wait_ge(even_copied, (part + 1) * (4 * RT) + START)
            pe.wait_ge(odd_copied, (part + 1) * (3 * RT) + START)

            def score(pair, b, t, first=False):
                before = (part * D + pair * 2 + b)
                if t == 0:
                    pe.wait_ge(qk_loaded[b], (part * HALF + pair + 1) * (16 * BATCH_DMAS))
                if t >= SLOTS:
                    holder, batches = t - SLOTS, before
                else:
                    holder, batches = (NT - 1) // SLOTS * SLOTS + t, before - 1
                    holder -= SLOTS if holder >= NT else 0
                if not (first and t < SLOTS):
                    if path.kind[holder] == "d":
                        pe.wait_ge(biased, batches * nd + path.before(holder, "d") + 1 + START)
                    else:
                        pe.wait_ge(exped, batches * NT + path.exped_with(holder))
                for a, w in SEGS:
                    last = nc.tensor.matmul(scores[:, t % SLOTS, a:a + w], keys[b][:, t * P:(t + 1) * P],
                                            queries[b][:, a:a + w], start=True, stop=True)
                last.then_inc(scored, 1)

            def weigh(pair, b, k):
                before = (part * D + pair * 2 + b)
                t = path.order[k]
                if k == 0:
                    pe.wait_ge(v_loaded[b], (part * HALF + pair + 1) * 16)
                    pe.wait_ge(acc_free[b], part * HALF + pair + 1)
                if path.kind[t] == "d":
                    pe.wait_ge(exped, before * NT + path.exped_with(t))
                    e = xd[(b * nd + path.before(t, "d")) % XD]
                else:
                    pe.wait_ge(factored, before * ng + path.before(t, "g") + 1 + START)
                    e = xg[(b * ng + path.before(t, "g")) % XG]
                for c in range(CH):
                    w = CHS[c + 1] - CHS[c]
                    last = nc.tensor.matmul(acc[32 * c:32 * c + VC, b, 0:w], values[b][:, t * VC:(t + 1) * VC],
                                            e[:, CHS[c]:CHS[c + 1]], start=(k == 0), stop=(k == NT - 1),
                                            tile_position=(0, 32 * c))
                last.then_inc(weighed, 1)

            AHEAD = 5
            steps = [(b, t) for b in range(2) for t in range(NT)]
            for t in range(AHEAD):
                score(0, 0, t, first=True)
            with pe.Fori(0, HALF - 1) as pair:
                for s, (b, k) in enumerate(steps):
                    nxt = s + AHEAD
                    if nxt < len(steps):
                        score(pair, *steps[nxt])
                    else:
                        score(pair + 1, *steps[nxt - len(steps)])
                    weigh(pair, b, k)
            for s, (b, k) in enumerate(steps):
                if s + AHEAD < len(steps):
                    score(HALF - 1, *steps[s + AHEAD])
                weigh(HALF - 1, b, k)

    def vector(dve):
        amax = small[:, 0:2]
        with dve.Fori(0, PARTS) as part:
            dve.wait_ge(factored, part * (ng * D) + START)
            dve.wait_ge(biased, part * (nd * D) + START)

            def copy_groups(j):
                tile = part * RT + j
                for k, (t0, n) in enumerate(GROUPS):
                    if k % 2 == 0:
                        dve.wait_ge(turned, tile * len(GROUPS) + k + 1 + START)
                        copy_group(nc.vector.tensor_copy, j, k, t0, n).then_inc(even_copied, 1)

            for j in range(RT):
                rows = rows_of[j]
                tile = part * RT + j
                dve.wait_ge(nat_loaded[j % 2], natural_count(part, j) * 16)
                nc.vector.reduce_max(amax[0:rows, j % 2:j % 2 + 1], nat[j % 2][0:rows, :], AX.X).then_inc(row_max, 1)
                dve.wait_ge(row_max, tile + 1)
                nc.vector.tensor_scalar(nat[j % 2][0:rows, :], nat[j % 2][0:rows, :], amax[0:rows, j % 2:j % 2 + 1], 2.0,
                                        ALU.subtract, ALU.mult).then_inc(nat_ready, 1)
                if j:
                    copy_groups(j - 1)
            copy_groups(RT - 1)
            if not path.factored:
                find_maxima_vector(dve, part)
            with dve.Fori(0, HALF) as pair:
                dve.wait_ge(even_copied, (part + 1) * (4 * RT) + START)
                dve.wait_ge(odd_copied, (part + 1) * (3 * RT) + START)
                for b in range(2):
                    before = part * D + pair * 2 + b
                    for t in range(NT):
                        if path.kind[t] != "d":
                            continue
                        n = path.before(t, "d")
                        dve.wait_ge(scored, before * NT + t + 1 + CREDIT)
                        dve.wait_ge(weighed, before * NT + path.weighed_since(n, "d", XD) + CREDIT)
                        nc.vector.tensor_tensor(xd[(b * nd + n) % XD][:, :], scores[:, t % SLOTS, 0:W], bias[:, t, :],
                                                ALU.add).then_inc(biased, 1)

    def copy_group(copy, j, k, t0, n):
        rows = rows_of[j]
        bank = banks[:, k % 6, :].rearrange("p (t c) -> p t c", c=P)
        if t0 + n < NT:
            return copy(bias[:, t0:t0 + n, j * P:j * P + rows], bank[:, 0:n, 0:rows])
        copy(bias[:, t0:t0 + n - 1, j * P:j * P + rows], bank[:, 0:n - 1, 0:rows])
        return copy(bias[0:LAST, NT - 1, j * P:j * P + rows], bank[0:LAST, n - 1, 0:rows])

    def scalar(act):
        with act.Fori(0, PARTS) as part:
            act.wait_ge(factored, part * (ng * D) + START)
            act.wait_ge(biased, part * (nd * D) + START)

            def copy_groups(j):
                tile = part * RT + j
                for k, (t0, n) in enumerate(GROUPS):
                    if k % 2:
                        act.wait_ge(turned, tile * len(GROUPS) + k + 1 + START)
                        copy_group(nc.scalar.copy, j, k, t0, n).then_inc(odd_copied, 1)

            for j in range(RT):
                if path.factored:
                    act.wait_ge(nat_ready, part * RT + j + 1)
                    nc.scalar.activation(gview(rows_of[j], j % 2), gview(rows_of[j], j % 2), ACT.Exp).then_inc(nat_exp, 1)
                if j:
                    copy_groups(j - 1)
            copy_groups(RT - 1)

            def take(pair, b):
                act.wait_ge(weighed, (part * D + pair * 2 + b + 1) * NT + CREDIT)
                act.wait_ge(out_stored[b], (part * HALF + pair) * (16 * CH) + START)
                nc.scalar.copy(attended[b][0:96 + VC, :], acc[0:96 + VC, b, 0:CHW]).then_inc(acc_free[b], 1)

            def batch(pair, b, previous):
                before = part * D + pair * 2 + b
                for t in path.exp_order:
                    if t == 6 and previous is not None:
                        take(*previous)
                    if path.kind[t] == "d":
                        n = path.before(t, "d")
                        act.wait_ge(biased, before * nd + n + 1 + START)
                        e = xd[(b * nd + n) % XD]
                        nc.scalar.activation(e[:, :], e[:, :], ACT.Exp).then_inc(exped, 1)
                    else:
                        n = path.before(t, "g")
                        act.wait_ge(scored, before * NT + t + 1 + CREDIT)
                        act.wait_ge(weighed, before * NT + path.weighed_since(n, "g", XG) + CREDIT)
                        nc.scalar.activation(xg[(b * ng + n) % XG][:, :], scores[:, t % SLOTS, 0:W],
                                             ACT.Exp).then_inc(exped, 1)

            batch(0, 0, None)
            batch(0, 1, (0, 0))
            with act.Fori(1, HALF) as pair:
                batch(pair, 0, (pair - 1, 1))
                batch(pair, 1, (pair, 0))
            take(HALF - 1, 1)

    def gpsimd(pool):
        if not path.factored:
            return
        with pool.Fori(0, PARTS) as part:
            with pool.Fori(0, HALF) as pair:
                pool.wait_ge(even_copied, (part + 1) * (4 * RT) + START)
                pool.wait_ge(odd_copied, (part + 1) * (3 * RT) + START)
                for b in range(2):
                    before = part * D + pair * 2 + b
                    for t in range(NT):
                        if path.kind[t] != "g":
                            continue
                        e = xg[(b * ng + path.before(t, "g")) % XG]
                        pool.wait_ge(exped, before * NT + path.exped_with(t))
                        nc.gpsimd.tensor_tensor(e[:, :], e[:, :], bias[:, t, :], ALU.mult).then_inc(factored, 1)

    run, trial = xd[0], xd[1]
    cmax = small[:, 8:8 + RT]
    cneg = small[0:RT, 32:32 + P]
    crest = small[0:RT, 160:160 + P]
    cpiece = small[0:RT, 288:288 + SPLIT * P // 2].bitcast(bf16).rearrange("r (s n) -> r s n", s=SPLIT)
    if not path.factored:
        m_loaded, m_scored, m_added, m_run = (sem(f"max_{s}") for s in ("loaded", "scored", "added", "run"))
        m_turned, m_column, m_row, m_chain = (sem(f"max_{s}") for s in ("turned", "column", "row", "chain"))
        m_ready, m_stored, m_zeroed = sem("max_ready"), sem("max_stored"), sem("max_zeroed")

    def find_maxima_sync(sp, part):
        with sp.Fori(0, D) as d:
            seen = part * D + d
            sp.wait_ge(scored, part * (D * NT) + CREDIT)
            sp.wait_ge(m_scored, seen * NT + START)
            load_batch(sp, d, part, 0, m_loaded, shifted=False)
            sp.wait_ge(m_ready, seen + 1)
            at = d * N + part * STEP
            sp.dma_start(shift_d[:, bass.ds(at, (RT - 1) * P)].rearrange("s (r n) -> r s n", n=P),
                         cpiece[0:RT - 1]).then_inc(m_stored, 16)
            sp.dma_start(shift_d[:, bass.ds(at + (RT - 1) * P, RLAST)].unsqueeze(0),
                         cpiece[RT - 1:RT, :, 0:RLAST]).then_inc(m_stored, 16)
        sp.wait_ge(m_stored, (part + 1) * (D * 32) + START)

    def find_maxima_tensor(pe, part):
        with pe.Fori(0, D) as d:
            seen = part * D + d
            pe.wait_ge(even_copied, (part + 1) * (4 * RT) + START)
            pe.wait_ge(odd_copied, (part + 1) * (3 * RT) + START)
            pe.wait_ge(m_loaded, (seen + 1) * (16 * 2 * SPLIT))
            pe.wait_ge(m_zeroed, part + 1)
            for t in range(NT):
                pe.wait_ge(m_added, seen * NT + max(t - SLOTS + 1, 0) + START)
                for a, w in SEGS:
                    last = nc.tensor.matmul(scores[:, t % SLOTS, a:a + w], keys[0][:, t * P:(t + 1) * P],
                                            queries[0][:, a:a + w], start=True, stop=True)
                last.then_inc(m_scored, 1)
            pe.wait_ge(m_run, (seen + 1) * NT + START)
            for r in range(RT):
                w = rows_of[r]
                last = nc.tensor.transpose(banks[0:w, r // 4, P * (r % 4):P * (r % 4 + 1)], run[:, r * P:r * P + w],
                                           ident[:, :])
            last.then_inc(m_turned, 1)
            pe.wait_ge(m_column, seen + 1)
            nc.tensor.transpose(acc[0:RT, 0, 0:P], cmax, ident[:, :]).then_inc(m_row, 1)

    def find_maxima_vector(dve, part):
        LINKS = 5
        dve.wait_ge(scored, part * (D * NT) + CREDIT)
        nc.vector.memset(queries[0][0:SPLIT, :], 0.0).then_inc(m_zeroed, 1)
        with dve.Fori(0, D) as d:
            seen = part * D + d
            links = [0]
            dve.wait_ge(even_copied, (part + 1) * (4 * RT) + START)
            dve.wait_ge(odd_copied, (part + 1) * (3 * RT) + START)
            dve.wait_ge(weighed, part * (D * NT) + CREDIT)
            dve.wait_ge(m_stored, seen * 32 + START)

            def link(ins):
                links[0] += 1
                ins.then_inc(m_chain, 1)
                dve.wait_ge(m_chain, seen * LINKS + links[0])

            link(nc.vector.memset(run[:, :], -3.0e38))
            for t in range(NT):
                dve.wait_ge(m_scored, seen * NT + t + 1 + START)
                dve.wait_ge(m_run, seen * NT + t + START)
                nc.vector.tensor_tensor(trial[:, :], scores[:, t % SLOTS, 0:W], bias[:, t, :], ALU.add).then_inc(m_added, 1)
                dve.wait_ge(m_added, seen * NT + t + 1 + START)
                nc.vector.tensor_tensor(run[:, :], run[:, :], trial[:, :], ALU.max).then_inc(m_run, 1)
            dve.wait_ge(m_turned, seen + 1)
            link(nc.vector.memset(cmax, 0.0))
            nc.vector.tensor_reduce(cmax[:, 0:RT - 1], flatp[:, 0:(RT - 1) * P].rearrange("p (r n) -> p r n", n=P), AX.X,
                                    ALU.max, negate=True)
            nc.vector.tensor_reduce(cmax[0:RLAST, RT - 1:RT], flatp[0:RLAST, (RT - 1) * P:RT * P], AX.X, ALU.max,
                                    negate=True).then_inc(m_column, 1)
            dve.wait_ge(m_row, seen + 1)
            link(nc.vector.tensor_copy(cpiece[:, 0, :], acc[0:RT, 0, 0:P]))
            link(nc.vector.tensor_tensor(crest, acc[0:RT, 0, 0:P], cpiece[:, 0, :], ALU.subtract))
            link(nc.vector.tensor_copy(cpiece[:, 1, :], crest))
            nc.vector.tensor_tensor(cpiece[:, 2, :], crest, cpiece[:, 1, :], ALU.subtract).then_inc(m_ready, 1)
            assert links[0] == LINKS

    return {"sync": sync, "tensor": tensor, "vector": vector, "scalar": scalar, "gpsimd": gpsimd}


def value_band(v_d, first):
    flat = v_d.rearrange("y c -> (y c)")[bass.ds(first, P * VROW)]
    return flat.rearrange("(y c) -> y c", c=VROW)[:, 0:NT * VC]


def project(nc, sem, carve, x, wo, o_d, out, ident, banks, flatp, acc):
    wo_raw = carve(H * P)
    wo_t = carve(H * P).rearrange("p (h o) -> p h o", o=P)
    heads = [carve(VC * P).rearrange("p (h g) -> p h g", g=P) for _ in range(2)]
    heads_t = [carve(H * P).rearrange("p (h r) -> p h r", r=P) for _ in range(2)]
    recip = [carve(P) for _ in range(2)]
    x_in = [carve(P) for _ in range(2)]
    y = [carve(P) for _ in range(2)]
    o_rows = o_d.rearrange("h (r g) -> r h g", g=P)

    wo_loaded, wo_turned, wo_ready = sem("wo_loaded"), sem("wo_turned"), sem("wo_ready")
    loaded = [sem("heads_loaded0"), sem("heads_loaded1")]
    inverted, divided, turned, copied = sem("inverted"), sem("divided"), sem("heads_turned"), sem("heads_copied")
    summed, added = sem("summed"), sem("added")
    y_stored = [sem("y_stored0"), sem("y_stored1")]

    with nc.Block() as block:
        def all_tiles(engine, tile):
            with engine.Fori(0, NT // 2 - 1) as pair:
                for b in range(2):
                    tile(pair, b, P)
            for b in range(2):
                tile(NT // 2 - 1, b, LAST if b else P)

        @block.sync
        def _(sp):
            for s in (turned, added, copied, summed, *y_stored):
                sp.sem_inc(s, START)
            sp.dma_start(wo_raw, wo[:, :]).then_inc(wo_loaded, 16)

            def load(pair, b, rows):
                i = pair * 2 + b
                sp.wait_ge(turned, pair * 2 + START)
                sp.wait_ge(added, pair * 2 + START)
                sp.dma_start(heads[b], o_rows[bass.ds(i * P, P), :, :]).then_inc(loaded[b], 16)
                sp.dma_start(x_in[b][0:rows, :], x[bass.ds(i * P, rows), :]).then_inc(loaded[b], 16)

            def store(pair, b, rows):
                i = pair * 2 + b
                sp.wait_ge(added, i + 1 + START)
                sp.dma_start(out[bass.ds(i * P, rows), :], y[b][0:rows, :]).then_inc(y_stored[b], 16)

            for b in range(2):
                load(0, b, P)
            with sp.Fori(1, NT // 2 - 1) as pair:
                for b in range(2):
                    load(pair, b, P)
                    store(pair - 1, b, P)
            for b in range(2):
                load(NT // 2 - 1, b, LAST if b else P)
                store(NT // 2 - 2, b, P)
            for b in range(2):
                store(NT // 2 - 1, b, LAST if b else P)
            for b in range(2):
                sp.wait_ge(y_stored[b], 16 * (NT // 2) + START)

        @block.tensor
        def _(pe):
            pe.wait_ge(wo_loaded, 16)
            for h in range(H):
                last = nc.tensor.transpose(banks[:, h // 4, P * (h % 4):P * (h % 4 + 1)],
                                           wo_raw.rearrange("o (g h) -> o h g", h=H)[:, h, :], ident[:, :])
            last.then_inc(wo_turned, 1)
            pe.wait_ge(wo_ready, 1)

            def tile(pair, b, rows):
                i = pair * 2 + b
                pe.wait_ge(divided, i + 1)
                pe.wait_ge(copied, pair * 2 + START)
                for h in range(H):
                    last = nc.tensor.transpose(banks[:, 2 * b + h // 4, P * (h % 4):P * (h % 4 + 1)], heads[b][:, h, :],
                                               ident[:, :])
                last.then_inc(turned, 1)
                pe.wait_ge(copied, i + 1 + START)
                pe.wait_ge(added, pair * 2 + START)
                for h in range(H):
                    last = nc.tensor.matmul(acc[:, b, 0:P], heads_t[b][:, h, :], wo_t[:, h, :], start=(h == 0),
                                            stop=(h == H - 1))
                last.then_inc(summed, 1)

            all_tiles(pe, tile)

        @block.scalar
        def _(act):
            act.wait_ge(wo_turned, 1)
            nc.scalar.copy(wo_t.rearrange("p h o -> p (h o)"), flatp[:, 0:H * P]).then_inc(wo_ready, 1)

            def tile(pair, b, rows):
                i = pair * 2 + b
                act.wait_ge(turned, i + 1 + START)
                act.wait_ge(summed, pair * 2 + START)
                nc.scalar.copy(heads_t[b].rearrange("p h r -> p (h r)"),
                               flatp[:, 2 * b * BANK:2 * (b + 1) * BANK]).then_inc(copied, 1)

            all_tiles(act, tile)

        @block.vector
        def _(dve):
            def tile(pair, b, rows):
                i = pair * 2 + b
                dve.wait_ge(loaded[b], (pair + 1) * 32)
                nc.vector.reciprocal(recip[b][0:rows, :], heads[b][0:rows, H, :]).then_inc(inverted, 1)
                dve.wait_ge(inverted, i + 1)
                nc.vector.tensor_tensor(heads[b][0:rows, 0:H, :], heads[b][0:rows, 0:H, :],
                                        recip[b][0:rows, :].unsqueeze(1).to_broadcast([rows, H, P]),
                                        ALU.mult).then_inc(divided, 1)
                dve.wait_ge(summed, i + 1 + START)
                dve.wait_ge(y_stored[b], pair * 16 + START)
                nc.vector.tensor_tensor(y[b][0:rows, :], acc[0:rows, b, 0:P], x_in[b][0:rows, :],
                                        ALU.add).then_inc(added, 1)

            all_tiles(dve, tile)


_INS = ["x", "adj", "L0_gnn_Wq", "L0_gnn_Wk", "L0_gnn_Wv", "L0_gnn_Wo"]


def kernel(**inputs):
    import numpy as _np
    import concourse.bacc as _bacc
    from concourse import mybir as _mybir
    from concourse.bass_utils import run_bass_kernel_spmd as _run

    nc = _bacc.Bacc("TRN2", target_bir_lowering=False, num_devices=1)
    arrays, args = {}, []
    for name in _INS:
        a = _np.ascontiguousarray(inputs[name])
        arrays[f"in_{name}"] = a
        args.append(nc.dram_tensor(f"in_{name}", a.shape, _mybir.dt.from_np(a.dtype), kind="ExternalInput").ap())
    args.append(nc.dram_tensor("out", (N, D), fp32, kind="ExternalOutput").ap())
    build(nc, *args)
    r = _run(nc, [arrays], core_ids=[0])
    return r.results[0]["out"]
```

```python
from contextlib import ExitStack

import concourse.bass as bass
from concourse import mybir

N = 3327
D = 128
H = 8
P = 128
NT = (N + P - 1) // P
NPAD = NT * P
LAST = N - (NT - 1) * P
FLAT = NPAD * P
PARTS = 4
STEP = N // PARTS
W = N - (PARTS - 1) * STEP
RT = (W + P - 1) // P
RLAST = W - (RT - 1) * P
CH = 4
CHS = [W * c // CH for c in range(CH + 1)]
CHW = max(CHS[c + 1] - CHS[c] for c in range(CH))
VC = H + 1
SPLIT = 3
KR = SPLIT + SPLIT * SPLIT * H
SCALE = float(D) ** -0.5
EPS = 1e-5
MASKED = -1.0e30
SAFE = 34.0
BANK = 512
SLOTS = 3
START = 1
VROW = (NPAD + 1) * VC
RING = 3
XD, XG = 11, 3
ARENA = max(240 * P, (NT + XD + XG) * W)
GROUPS = [(4 * k, min(4, NT - 4 * k)) for k in range((NT + 3) // 4)]
SEGS = [(a, min(BANK, W - a)) for a in range(0, W, BANK)]

fp32 = mybir.dt.float32
bf16 = mybir.dt.bfloat16
i32 = mybir.dt.int32
ALU = mybir.AluOpType
ACT = mybir.ActivationFunctionType
AX = mybir.AxisListType


def build(nc, x, adj, wq, wk, wv, wo, out):
    qk_d = nc.dram_tensor("qk_pieces", [SPLIT, 2, H, FLAT], bf16).ap()
    shift_d = nc.dram_tensor("shift_pieces", [SPLIT, FLAT], bf16).ap()
    qnorm_d = nc.dram_tensor("qnorm", [FLAT], fp32).ap()
    v_d = nc.dram_tensor("values", [2 * P, VROW], fp32).ap()
    o_d = nc.dram_tensor("attended", [VC, FLAT], fp32).ap()

    ctx = ExitStack()
    with ctx:
        def sb(name, shape, dt=fp32):
            return ctx.enter_context(nc.sbuf_tensor(name, shape, dt))

        def sem(name):
            return ctx.enter_context(nc.semaphore(name))

        arena = sb("arena", [P, ARENA])
        bias = arena[:, 0:NT * W].rearrange("p (t n) -> p t n", n=W)
        room = arena[:, :]
        used = [0]

        def carve(cols, dt=fp32):
            a = used[0]
            used[0] = a + cols
            v = room[:, a:a + cols]
            return v if dt == fp32 else v.bitcast(dt)

        nat = [sb(f"nat{b}", [P, N]) for b in range(2)]
        keys = [sb(f"keys{b}", [KR, NPAD], bf16) for b in range(2)]
        queries = [sb(f"queries{b}", [KR, W], bf16) for b in range(2)]
        values = [sb(f"values{b}", [P, NT * VC]) for b in range(2)]
        xd = arena[:, NT * W:(NT + XD) * W].rearrange("p (b n) -> p b n", n=W)
        xg = arena[:, (NT + XD) * W:(NT + XD + XG) * W].rearrange("p (b n) -> p b n", n=W)
        assert 2 * N <= (XD + XG) * W
        nat_more = [arena[:, NT * W + b * N:NT * W + (b + 1) * N] for b in range(2)]
        attended = [sb(f"attended_sb{b}", [P, CHW]) for b in range(2)]
        ident = sb("ident", [P, P])
        small = sb("small", [P, 512])
        flag = sb("flag", [P, 1], i32)

        scores = ctx.enter_context(nc.psum_tensor("scores", [P, SLOTS, 2 * BANK], fp32))
        acc = ctx.enter_context(nc.psum_tensor("acc", [P, 2, BANK], fp32))
        banks = scores[:, :, :].rearrange("p a (b n) -> p (a b) n", n=BANK)
        flatp = scores[:, :, :].rearrange("p a n -> p (a n)")

        prepare(nc, ctx, sem, carve, x, wq, wk, wv, qk_d, qnorm_d, v_d, o_d, shift_d, nat, keys, ident, small, flag,
                banks, flatp, acc)
        attend(nc, sem, adj, qk_d, shift_d, v_d, o_d, bias, nat + nat_more, keys, queries, values, xd, xg, attended, ident,
               small, flag, scores, banks, flatp, acc)
        used[0] = 0
        project(nc, sem, carve, x, wo, o_d, out, ident, banks, flatp, acc)


def prepare(nc, ctx, sem, carve, x, wq, wk, wv, qk_d, qnorm_d, v_d, o_d, shift_d, nat, keys, ident, small, flag,
            banks, flatp, acc):
    x_all = carve(NT * P).rearrange("p (t c) -> p t c", c=P)
    sq_all = carve(NT * P).rearrange("p (t c) -> p t c", c=P)
    w_raw = [carve(H * P).rearrange("p (h c) -> p h c", c=P) for _ in range(3)]
    w_t = [carve(H * P).rearrange("p (h g) -> p h g", g=P) for _ in range(3)]
    h_row = [carve(P) for _ in range(2)]
    h_t = [carve(P) for _ in range(2)]
    pieces = [carve(SPLIT * 2 * H * P // 2, bf16).rearrange("p (s m n) -> p s m n", s=SPLIT, m=2) for _ in range(2)]
    rest = [carve(H * P) for _ in range(4)]
    square = [carve(H * P) for _ in range(2)]
    v_out = [carve(P * VC).rearrange("p (r h) -> p r h", h=VC) for _ in range(2)]
    norm = [carve(2 * P).rearrange("p (m g) -> p m g", m=2) for _ in range(2)]
    top = carve(2 * P).rearrange("p (m g) -> p m g", m=2)

    mean, var, root, inv = (small[:, 32 * i:32 * i + NT] for i in range(4))
    half = small[:, 128:128 + NT]
    peak, peaks, bound, safe, keep, negkeep = (small[:, 160 + 2 * i:162 + 2 * i] for i in range(6))

    x_padded, x_loaded, w_loaded = sem("x_padded"), sem("x_loaded"), sem("w_loaded")
    filled, ident_ready, w_turned, w_ready = sem("filled"), sem("ident_ready"), sem("w_turned"), sem("w_ready")
    chain, var_ready, root_ready, ln_done = sem("chain"), sem("var_ready"), sem("root_ready"), sem("ln_done")
    h_ready, h_turned, h_t_ready = sem("h_ready"), sem("h_turned"), sem("h_t_ready")
    projected = [sem("q_projected"), sem("k_projected"), sem("v_projected")]
    first_piece = [sem("q_first"), sem("k_first")]
    squared = [sem("q_squared"), sem("k_squared")]
    rest_ready = [sem("q_rest"), sem("k_rest")]
    normed = [sem("q_normed"), sem("k_normed")]
    second_piece = [sem("q_second"), sem("k_second")]
    third_piece = [sem("q_third"), sem("k_third")]
    v_ready, norm_kept = sem("v_ready"), sem("norm_kept")
    stored = [sem("pieces_stored0"), sem("pieces_stored1")]
    v_stored = [sem("v_stored0"), sem("v_stored1")]
    peak_ready, peaks_ready, safe_ready = sem("peak_ready"), sem("peaks_ready"), sem("safe_ready")
    norms_loaded, clamped, shift_root = sem("norms_loaded"), sem("clamped"), sem("shift_root")
    shift_ready, shift_stored, pad_stored = sem("shift_ready"), sem("shift_stored"), sem("pad_stored")
    seconds_ready = sem("seconds_ready")

    shift = nat[0]
    shift_rest = nat[1]

    qk_rows = qk_d.rearrange("s m h (r g) -> r (s m h) g", g=P)
    norm_rows = qnorm_d.rearrange("(r g) -> r g", g=P)
    sp_pieces = sq_all.rearrange("p t c -> p (t c)")
    x_pieces = x_all.rearrange("p t c -> p (t c)")
    piece_a = sp_pieces.bitcast(bf16)[:, 0:N]
    piece_b = sp_pieces.bitcast(bf16)[:, NPAD:NPAD + N]
    piece_c = x_pieces.bitcast(bf16)[:, 0:N]

    with nc.Block() as block:
        @block.sync
        def _(sp):
            for s in (h_t_ready, h_turned, v_ready, projected[2], *squared, *rest_ready, *normed, *second_piece, *third_piece,
                      *stored, *v_stored):
                sp.sem_inc(s, START)
            sp.dma_start(x_all[:, 0:NT - 1, :],
                         x[0:(NT - 1) * P, :].rearrange("(t p) c -> p t c", p=P)).then_inc(x_loaded, 16)
            sp.wait_ge(x_padded, 1)
            sp.dma_start(x_all[0:LAST, NT - 1, :], x[(NT - 1) * P:N, :]).then_inc(x_loaded, 16)
            for m, w in enumerate((wq, wk, wv)):
                sp.dma_start(w_raw[m], w.rearrange("(g h) c -> g h c", h=H)).then_inc(w_loaded, 16)
            with sp.Fori(0, NT // 2) as pair:
                for b in range(2):
                    i = pair * 2 + b
                    for m in range(2):
                        sp.wait_ge(second_piece[m], i + 1 + START)
                        sp.wait_ge(third_piece[m], i + 1 + START)
                    sp.wait_ge(normed[0], i + 1 + START)
                    sp.dma_start(qk_rows[bass.ds(i * P, P), :, :],
                                 pieces[b].rearrange("p s m (h g) -> p (s m h) g", g=P)).then_inc(stored[b], 16)
                    sp.dma_start(norm_rows[bass.ds(i * P, P), :], norm[b][:, 0, :]).then_inc(stored[b], 16)
                    sp.wait_ge(v_ready, i + 1 + START)
                    sp.dma_start(v_d[P:2 * P, bass.ds(i * (P * VC), P * VC)],
                                 v_out[b].rearrange("p r h -> p (r h)")).then_inc(v_stored[b], 16)
                    sp.dma_start(v_d[0:P, bass.ds(i * (P * VC) + VC, P * VC)],
                                 v_out[b].rearrange("p r h -> p (r h)")).then_inc(v_stored[b], 16)
            sp.wait_ge(filled, 1)
            sp.dma_start(o_d[:, N * P:FLAT], small[0:VC, 256:256 + P]).then_inc(pad_stored, 16)
            for b in range(2):
                sp.wait_ge(stored[b], 32 * (NT // 2) + START)
                sp.wait_ge(v_stored[b], 32 * (NT // 2) + START)
            sp.dma_start(shift[:, :], qnorm_d[0:N * D].rearrange("(d n) -> d n", n=N)).then_inc(norms_loaded, 16)
            sp.wait_ge(shift_ready, 1)
            sp.wait_ge(seconds_ready, 1)
            for s, piece in enumerate((piece_a, piece_b, piece_c)):
                sp.dma_start(shift_d[s, 0:N * D].rearrange("(d n) -> d n", n=N), piece).then_inc(shift_stored, 16)
            sp.dma_start(shift_d[:, N * D:FLAT], small[0:SPLIT, 384:384 + P // 2].bitcast(bf16)).then_inc(shift_stored, 16)
            sp.wait_ge(shift_stored, 64)
            sp.wait_ge(pad_stored, 16)

        @block.gpsimd
        def _(pool):
            nc.gpsimd.memset(small[:, 256:384], 1.0)
            nc.gpsimd.memset(small[:, 384:512], 0.0).then_inc(filled, 1)
            nc.gpsimd.memset(ident[:, :], 0.0).then_inc(ident_ready, 1)
            pool.wait_ge(ident_ready, 1)
            nc.gpsimd.affine_select(out=ident[:, :], in_=ident[:, :], compare_op=ALU.not_equal, fill=1.0, base=0,
                                    pattern=[[-1, P]], channel_multiplier=1).then_inc(ident_ready, 1)
            with pool.Fori(0, NT // 2) as pair:
                for b in range(2):
                    i = pair * 2 + b
                    for m in range(2):
                        pool.wait_ge(second_piece[m], i + 1 + START)
                        nc.gpsimd.tensor_tensor(pieces[b][:, 2, m, :], rest[2 * b + m], pieces[b][:, 1, m, :],
                                                ALU.subtract).then_inc(third_piece[m], 1)
            pool.wait_ge(peak_ready, 1)
            nc.gpsimd.partition_all_reduce(peaks, peak, P, bass.bass_isa.ReduceOp.max).then_inc(peaks_ready, 1)

        @block.tensor
        def _(pe):
            pe.wait_ge(ident_ready, 2)
            pe.wait_ge(w_loaded, 48)
            for m in range(3):
                for h in range(H):
                    last = nc.tensor.transpose(banks[:, 2 * m + h // 4, P * (h % 4):P * (h % 4 + 1)],
                                               w_raw[m][:, h, :], ident[:, :])
                last.then_inc(w_turned, 1)
            with pe.Fori(0, NT // 2) as pair:
                for b in range(2):
                    i = pair * 2 + b
                    pe.wait_ge(h_ready, i + 1)
                    pe.wait_ge(h_t_ready, i + START)
                    nc.tensor.transpose(acc[:, 0, 0:P], h_row[b], ident[:, :]).then_inc(h_turned, 1)
                    pe.wait_ge(h_t_ready, i + 1 + START)
                    if b == 0:
                        pe.wait_ge(w_ready, 3)
                    for m in range(2):
                        pe.wait_ge(squared[m], i + START)
                        pe.wait_ge(rest_ready[m], i + START)
                        for s in range(2):
                            last = nc.tensor.matmul(banks[:, 2 * m + s, :], h_t[b],
                                                    w_t[m][:, 4 * s:4 * s + 4, :].rearrange("p h g -> p (h g)"),
                                                    start=True, stop=True)
                        last.then_inc(projected[m], 1)
                    pe.wait_ge(v_ready, i + START)
                    for h in range(H):
                        last = nc.tensor.matmul(banks[:, 4 + h // 4, P * (h % 4):P * (h % 4 + 1)], w_t[2][:, h, :],
                                                h_t[b], start=True, stop=True)
                    last.then_inc(projected[2], 1)

        @block.scalar
        def _(act):
            act.wait_ge(var_ready, 1)
            nc.scalar.activation(root, var, ACT.Sqrt).then_inc(root_ready, 1)
            for m in range(3):
                act.wait_ge(w_turned, m + 1)
                nc.scalar.copy(w_t[m].rearrange("p h g -> p (h g)"),
                               flatp[:, 2 * m * BANK:2 * (m + 1) * BANK]).then_inc(w_ready, 1)
            with act.Fori(0, NT // 2) as pair:
                for b in range(2):
                    i = pair * 2 + b
                    act.wait_ge(h_turned, i + 1 + START)
                    act.wait_ge(projected[2], pair * 2 + START)
                    nc.scalar.copy(h_t[b], acc[:, 0, 0:P]).then_inc(h_t_ready, 1)
                    act.wait_ge(stored[b], pair * 32 + START)
                    for m in range(2):
                        src = flatp[:, 2 * m * BANK:2 * (m + 1) * BANK]
                        scale = SCALE if m == 0 else 1.0
                        act.wait_ge(projected[m], i + 1)
                        nc.scalar.activation(pieces[b][:, 0, m, :], src, ACT.Copy, scale=scale).then_inc(first_piece[m], 1)
                        act.wait_ge(normed[m], i + START)
                        nc.scalar.activation(square[m], src, ACT.Square, scale=scale).then_inc(squared[m], 1)
                    for m in range(2):
                        act.wait_ge(rest_ready[m], i + 1 + START)
                        nc.scalar.copy(pieces[b][:, 1, m, :], rest[2 * b + m]).then_inc(second_piece[m], 1)
            act.wait_ge(clamped, 1)
            nc.scalar.activation(shift[:, :], shift[:, :], ACT.Sqrt).then_inc(shift_root, 1)
            act.wait_ge(shift_ready, 1)

        @block.vector
        def _(dve):
            links = [0]

            def link(ins):
                links[0] += 1
                ins.then_inc(chain, 1)
                dve.wait_ge(chain, links[0])

            nc.vector.memset(x_all[:, NT - 1, :], 0.0).then_inc(x_padded, 1)
            nc.vector.memset(top, 0.0)
            for b in range(2):
                nc.vector.memset(v_out[b], 1.0)
            link(nc.vector.memset(acc[:, :, :], 0.0))
            dve.wait_ge(x_loaded, 32)
            link(nc.vector.reduce_sum(mean, x_all, axis=AX.X))
            link(nc.vector.tensor_scalar(mean, mean, 1.0 / D, None, ALU.mult))
            link(nc.vector.tensor_tensor(x_all, x_all, mean.unsqueeze(2).to_broadcast([P, NT, P]), ALU.subtract))
            link(nc.vector.tensor_tensor(sq_all, x_all, x_all, ALU.mult))
            link(nc.vector.reduce_sum(var, sq_all, axis=AX.X))
            nc.vector.tensor_scalar(var, var, 1.0 / D, EPS, ALU.mult, ALU.add).then_inc(var_ready, 1)
            dve.wait_ge(var_ready, 1)
            dve.wait_ge(root_ready, 1)
            link(nc.vector.reciprocal(inv, root))
            link(nc.vector.tensor_tensor(half, var, inv, ALU.mult))
            link(nc.vector.tensor_tensor(half, half, root, ALU.add))
            link(nc.vector.tensor_scalar(half, half, 0.5, None, ALU.mult))
            link(nc.vector.reciprocal(inv, half))
            link(nc.vector.tensor_tensor(x_all, x_all, inv.unsqueeze(2).to_broadcast([P, NT, P]), ALU.mult))
            with dve.Fori(0, NT // 2) as pair:
                for b in range(2):
                    i = pair * 2 + b
                    dve.wait_ge(h_turned, pair * 2 + START)
                    nc.vector.tensor_scalar(h_row[b], x_all[:, bass.ds(i, 1), :].rearrange("p o c -> p (o c)"), 0.0,
                                            None, ALU.max).then_inc(h_ready, 1)
                    for m in range(2):
                        src = flatp[:, 2 * m * BANK:2 * (m + 1) * BANK]
                        dve.wait_ge(first_piece[m], i + 1)
                        dve.wait_ge(third_piece[m], pair * 2 + START)
                        dve.wait_ge(squared[m], i + 1 + START)
                        nc.vector.scalar_tensor_tensor(rest[2 * b + m], src, SCALE if m == 0 else 1.0,
                                                       pieces[b][:, 0, m, :], ALU.mult,
                                                       ALU.subtract).then_inc(rest_ready[m], 1)
                        dve.wait_ge(stored[b], pair * 32 + START)
                        nc.vector.reduce_sum(norm[b][:, m, :], square[m].rearrange("p (h g) -> p g h", g=P),
                                             axis=AX.X).then_inc(normed[m], 1)
                    dve.wait_ge(projected[2], i + 1 + START)
                    dve.wait_ge(v_stored[b], pair * 32 + START)
                    nc.vector.tensor_copy(v_out[b][:, :, 0:H],
                                          flatp[:, 4 * BANK:6 * BANK].rearrange("p (h r) -> p r h", r=P)).then_inc(v_ready, 1)
                    dve.wait_ge(normed[1], i + 1 + START)
                    nc.vector.tensor_tensor(top, top, norm[b], ALU.max).then_inc(norm_kept, 1)
                    dve.wait_ge(norm_kept, i + 1)
            link(nc.vector.tensor_reduce(peak, top, AX.X, ALU.max))
            nc.vector.tensor_copy(peak, peak).then_inc(peak_ready, 1)
            dve.wait_ge(peaks_ready, 1)
            link(nc.vector.tensor_tensor(bound[:, 0:1], peaks[:, 0:1], peaks[:, 1:2], ALU.mult))
            link(nc.vector.tensor_scalar(keep[:, 0:1], bound[:, 0:1], SAFE * SAFE, None, ALU.is_le))
            nc.vector.tensor_copy(flag[:, :], keep[:, 0:1])
            link(nc.vector.tensor_scalar(negkeep[:, 0:1], keep[:, 0:1], -1.0, None, ALU.mult))
            dve.wait_ge(norms_loaded, 16)
            nc.vector.tensor_scalar(shift[:, :], shift[:, :], peaks[:, 1:2], 1e-30, ALU.mult, ALU.max).then_inc(clamped, 1)
            dve.wait_ge(shift_root, 1)
            link(nc.vector.tensor_scalar(shift[:, :], shift[:, :], negkeep[:, 0:1], None, ALU.mult))
            link(nc.vector.tensor_copy(piece_a, shift[:, :]))
            link(nc.vector.tensor_tensor(shift_rest[:, :], shift[:, :], piece_a, ALU.subtract))
            nc.vector.tensor_copy(piece_b, shift_rest[:, :]).then_inc(seconds_ready, 1)
            dve.wait_ge(seconds_ready, 1)
            nc.vector.tensor_tensor(piece_c, shift_rest[:, :], piece_b, ALU.subtract).then_inc(shift_ready, 1)


class Path:

    def __init__(self, name, factored):
        self.name = name
        self.factored = factored
        self.kind = ["g" if factored and t % 4 == 3 else "d" for t in range(NT)]
        self.skip = 13
        assert (NT + 1) % SLOTS == 0
        self.nd, self.ng = self.kind.count("d"), self.kind.count("g")
        self.order = sorted(range(NT), key=lambda t: t + (2 if self.kind[t] == "g" else 0))
        self.group, self.ring = (3, RING) if factored else (2, 2)
        direct = [t for t in range(NT) if self.kind[t] == "d"]
        self.full = self.nd // self.group
        assert 2 * self.full % self.ring == 0
        self.groups = [tuple(direct[n:n + self.group]) for n in range(0, self.nd, self.group)]
        self.exps = sorted(self.groups + [(t,) for t in range(NT) if self.kind[t] == "g"],
                           key=lambda unit: unit[-1] + ((-1.5) if self.kind[unit[0]] == "g" else (0)))
        self.ne = len(self.exps)

    def exped_with(self, t):
        return [t in unit for unit in self.exps].index(True) + 1

    def buffer(self, b, t):
        if self.kind[t] == "g":
            n, full = self.before(t, "g"), self.ng // RING * RING
            return (b * full + n) % RING if n < full else RING
        u = [t in group for group in self.groups].index(True)
        place = self.groups[u].index(t)
        return place + self.group * ((b * self.full + u) % self.ring if u < self.full else self.ring)

    def weighed_since(self, b, t):
        same = [u for u in range(NT) if self.kind[u] == self.kind[t]]
        for u in reversed([u for u in same if u < t]):
            if self.buffer(b, u) == self.buffer(b, t):
                return self.order.index(u) + 1
        for u in reversed(same):
            if self.buffer(1 - b, u) == self.buffer(b, t):
                return self.order.index(u) + 1 - NT

    def slot(self, t):
        return (t + (1 if t >= self.skip else 0)) % SLOTS

    def slot_holder(self, t):
        for ago, tiles in ((0, range(t)), (1, range(NT))):
            same = [u for u in tiles if self.slot(u) == self.slot(t)]
            if same:
                return same[-1], ago

    def before(self, t, kind):
        return self.kind[:t].count(kind)


def attend(nc, sem, adj, qk_d, shift_d, v_d, o_d, bias, nat, keys, queries, values, xd, xg, attended, ident, small,
           flag, scores, banks, flatp, acc):
    fast, general = Path("fast", True), Path("general", False)
    args = (adj, qk_d, shift_d, v_d, o_d, bias, nat, keys, queries, values, xd, xg, attended, ident, small, scores,
            banks, flatp, acc)
    programs = [attention_programs(nc, sem, path, *args) for path in (fast, general)]
    ready = sem("attention_constants")

    with nc.Block() as block:
        def either(engine, which):
            bounded = engine.value_load(flag[0:1, 0:1], min_val=0, max_val=1)
            with engine.If(bounded == 1):
                programs[0][which](engine)
            with engine.Else():
                programs[1][which](engine)

        @block.sync
        def _(sp):
            sp.wait_ge(ready, 1)
            either(sp, "sync")

        @block.gpsimd
        def _(pool):
            pool.wait_ge(ready, 1)
            either(pool, "gpsimd")

        @block.tensor
        def _(pe):
            pe.wait_ge(ready, 1)
            either(pe, "tensor")

        @block.scalar
        def _(act):
            act.wait_ge(ready, 1)
            either(act, "scalar")

        @block.vector
        def _(dve):
            for b in range(2):
                nc.vector.memset(keys[b][0:SPLIT, :], 1.0)
            nc.vector.memset(bias[96:P, NT - 1, :], MASKED)
            nc.vector.memset(acc[:, :, :], 0.0).then_inc(ready, 1)
            dve.wait_ge(ready, 1)
            either(dve, "vector")


def attention_programs(nc, sem, path, adj, qk_d, shift_d, v_d, o_d, bias, nat, keys, queries, values, xd, xg,
                       attended, ident, small, scores, banks, flatp, acc):
    name = path.name
    nd, ng, ne = path.nd, path.ng, path.ne

    nat_loaded = [sem(f"{name}_nat_loaded{b}") for b in range(4)]
    row_max, nat_ready, nat_exp = sem(f"{name}_row_max"), sem(f"{name}_nat_ready"), sem(f"{name}_nat_exp")
    turned, copied = sem(f"{name}_turned"), sem(f"{name}_copied")
    qk_loaded = [sem(f"{name}_qk_loaded{b}") for b in range(2)]
    v_loaded = [sem(f"{name}_v_loaded{b}") for b in range(2)]
    scored = sem(f"{name}_scored")
    biased = sem(f"{name}_biased")
    exped = sem(f"{name}_exped")
    factored = sem(f"{name}_factored")
    weighed = sem(f"{name}_weighed")
    acc_free = [sem(f"{name}_acc_free{b}") for b in range(2)]
    out_stored = [sem(f"{name}_out_stored{b}") for b in range(2)]
    CREDIT = NT + START
    HALF = D // 2

    gview = lambda rows, b: nat[b][0:rows, 0:24 * P].rearrange("p (a q c) -> p a q c", q=4, c=P)[:, :, 3, :]
    rows_of = [P] * (RT - 1) + [RLAST]
    loads_of = [len(range(b, RT, 4)) for b in range(4)]
    NG = len(GROUPS)

    def natural_count(part, j):
        return part * loads_of[j % 4] + j // 4 + 1

    def load_adjacency(sp, part, tiles):
        for j in tiles:
            if j in (2, 3):
                sp.wait_ge(weighed, part * (D * NT) + CREDIT)
            elif j >= 4:
                sp.wait_ge(turned, part * (RT * NG) + (j - 3) * NG + START)
            else:
                sp.wait_ge(turned, part * (RT * NG) + START)
            sp.dma_start(nat[j % 4][0:rows_of[j], :],
                         adj[bass.ds(part * STEP + j * P, rows_of[j]), :]).then_inc(nat_loaded[j % 4], 16)

    def load_batch(sp, d, part, b, loaded, shifted=True):
        for s in range(SPLIT):
            r = SPLIT + s * SPLIT * H
            sp.dma_start(keys[b][r:r + SPLIT * H, :], qk_d[:, 1, :, bass.ds(d * N, NPAD)]).then_inc(loaded, 16)
            sp.dma_start(queries[b][r:r + SPLIT * H, :],
                         qk_d[s, 0, :, bass.ds(d * N + part * STEP, W)].unsqueeze(0).to_broadcast([SPLIT, H, W])
                         ).then_inc(loaded, 16)
        if shifted:
            sp.dma_start(queries[b][0:SPLIT, :], shift_d[:, bass.ds(d * N + part * STEP, W)]).then_inc(loaded, 16)

    BATCH_DMAS = 2 * SPLIT + 1

    def sync(sp):
        for s, credit in ((scored, CREDIT), (weighed, CREDIT)):
            sp.sem_inc(s, credit)
        for s in (*acc_free, *out_stored, turned, biased, factored):
            sp.sem_inc(s, START)
        sp.sem_inc(copied, NG)
        if not path.factored:
            for s in (m_scored, m_added, m_run, m_stored):
                sp.sem_inc(s, START)

        def attend_part(part, last=False):

            def load(pair, b):
                d = pair * 2 + b
                done = (part * D + d) * NT
                sp.wait_ge(scored, done - NT + CREDIT)
                sp.wait_ge(weighed, done - NT + CREDIT)
                load_batch(sp, d, part, b, qk_loaded[b])
                first = P * VROW - d * (VROW - NT * VC)
                sp.dma_start(values[b][:, :], value_band(v_d, first)).then_inc(v_loaded[b], 16)

            def store(pair, b):
                d = pair * 2 + b
                sp.wait_ge(acc_free[b], part * HALF + pair + 2)
                for c in range(CH):
                    w = CHS[c + 1] - CHS[c]
                    sp.dma_start(o_d[:, bass.ds(d * N + part * STEP + CHS[c], w)],
                                 attended[b][32 * c:32 * c + VC, 0:w]).then_inc(out_stored[b], 16)

            load_adjacency(sp, part, range(2, 4))
            if not path.factored:
                load_adjacency(sp, part, range(4, RT))
                find_maxima_sync(sp, part)
            for b in range(2):
                load(0, b)
            if path.factored:
                load_adjacency(sp, part, range(4, RT))
            with sp.Fori(1, HALF) as pair:
                for b in range(2):
                    load(pair, b)
                    store(pair - 1, b)
            if not last:
                load_adjacency(sp, part + 1, range(2))
            for b in range(2):
                store(HALF - 1, b)

        load_adjacency(sp, 0, range(2))
        with sp.Fori(0, PARTS - 1) as part:
            attend_part(part)
        attend_part(PARTS - 1, last=True)
        for b in range(2):
            sp.wait_ge(out_stored[b], 16 * CH * HALF * PARTS + START)

    def tensor(pe):
        with pe.Fori(0, PARTS) as part:
            pe.wait_ge(biased, part * (nd * D) + START)
            for b in range(2):
                pe.wait_ge(acc_free[b], part * HALF + 1)
            for j in range(RT):
                rows = rows_of[j]
                tile = part * RT + j
                if path.factored:
                    pe.wait_ge(nat_exp, tile + 1)
                pe.wait_ge(nat_ready, tile + 1)
                for k, (t0, n) in enumerate(GROUPS):
                    pe.wait_ge(copied, tile * NG + k + 1)
                    for t in range(t0, t0 + n):
                        cols = min(P, N - t * P)
                        last = nc.tensor.transpose(group_bank(k)[0:cols, P * (t - t0):P * (t - t0) + rows],
                                                   nat[j % 4][0:rows, t * P:t * P + cols], ident[0:rows, 0:rows])
                    last.then_inc(turned, 1)
            if not path.factored:
                find_maxima_tensor(pe, part)
            pe.wait_ge(copied, (part + 1) * (NG * RT) + NG)

            def score(pair, b, t, first=False):
                before = (part * D + pair * 2 + b)
                if t == 0:
                    pe.wait_ge(qk_loaded[b], (part * HALF + pair + 1) * (16 * BATCH_DMAS))
                holder, batches = path.slot_holder(t)
                batches = before - batches
                if not (first and t < SLOTS):
                    if path.kind[holder] == "d":
                        pe.wait_ge(biased, batches * nd + path.before(holder, "d") + 1 + START)
                    else:
                        pe.wait_ge(exped, batches * ne + path.exped_with(holder))
                for a, w in SEGS:
                    last = nc.tensor.matmul(scores[:, path.slot(t), a:a + w], keys[b][:, t * P:(t + 1) * P],
                                            queries[b][:, a:a + w], start=True, stop=True)
                last.then_inc(scored, 1)

            def weigh(pair, b, k):
                before = (part * D + pair * 2 + b)
                t = path.order[k]
                if k == 0:
                    pe.wait_ge(v_loaded[b], (part * HALF + pair + 1) * 16)
                    pe.wait_ge(acc_free[b], part * HALF + pair + 1)
                if path.kind[t] == "d":
                    pe.wait_ge(exped, before * ne + path.exped_with(t))
                    e = xd[:, path.buffer(b, t), :]
                else:
                    pe.wait_ge(factored, before * ng + path.before(t, "g") + 1 + START)
                    e = xg[:, path.buffer(b, t), :]
                for c in range(CH):
                    w = CHS[c + 1] - CHS[c]
                    last = nc.tensor.matmul(acc[32 * c:32 * c + VC, b, 0:w], values[b][:, t * VC:(t + 1) * VC],
                                            e[:, CHS[c]:CHS[c + 1]], start=(k == 0), stop=(k == NT - 1),
                                            tile_position=(0, 32 * c))
                last.then_inc(weighed, 1)

            AHEAD = 9
            steps = [(b, t) for b in range(2) for t in range(NT)]
            for t in range(AHEAD):
                score(0, 0, t, first=True)
            with pe.Fori(0, HALF - 1) as pair:
                for s, (b, k) in enumerate(steps):
                    nxt = s + AHEAD
                    if nxt < len(steps):
                        score(pair, *steps[nxt])
                    else:
                        score(pair + 1, *steps[nxt - len(steps)])
                    weigh(pair, b, k)
            for s, (b, k) in enumerate(steps):
                if s + AHEAD < len(steps):
                    score(HALF - 1, *steps[s + AHEAD])
                weigh(HALF - 1, b, k)

    def vector(dve):
        amax = small[:, 0:4]
        with dve.Fori(0, PARTS) as part:
            for j in range(RT):
                rows = rows_of[j]
                tile = part * RT + j
                most = amax[0:rows, j % 4:j % 4 + 1]
                dve.wait_ge(nat_loaded[j % 4], natural_count(part, j) * 16)
                nc.vector.reduce_max(most, nat[j % 4][0:rows, :], AX.X).then_inc(row_max, 1)
                dve.wait_ge(row_max, tile + 1)
                nc.vector.tensor_scalar(nat[j % 4][0:rows, :], nat[j % 4][0:rows, :], most, 2.0,
                                        ALU.subtract, ALU.mult).then_inc(nat_ready, 1)
            if not path.factored:
                find_maxima_vector(dve, part)
            with dve.Fori(0, HALF) as pair:
                dve.wait_ge(copied, (part + 1) * (NG * RT) + NG)
                for b in range(2):
                    before = part * D + pair * 2 + b
                    for t in range(NT):
                        if path.kind[t] != "d":
                            continue
                        dve.wait_ge(scored, before * NT + t + 1 + CREDIT)
                        dve.wait_ge(weighed, before * NT + path.weighed_since(b, t) + CREDIT)
                        nc.vector.tensor_tensor(xd[:, path.buffer(b, t), :], scores[:, path.slot(t), 0:W], bias[:, t, :],
                                                ALU.add).then_inc(biased, 1)

    def group_bank(k):
        return banks[:, k, :] if k < 6 else acc[:, k - 6, :]

    def copy_group(copy, j, k, t0, n):
        rows = rows_of[j]
        bank = group_bank(k).rearrange("p (t c) -> p t c", c=P)
        if t0 + n < NT:
            return copy(bias[:, t0:t0 + n, j * P:j * P + rows], bank[:, 0:n, 0:rows])
        copy(bias[:, t0:t0 + n - 1, j * P:j * P + rows], bank[:, 0:n - 1, 0:rows])
        return copy(bias[0:LAST, NT - 1, j * P:j * P + rows], bank[0:LAST, n - 1, 0:rows])

    def scalar(act):
        def copy_groups(part, j):
            for k, (t0, n) in enumerate(GROUPS):
                act.wait_ge(turned, (part * RT + j) * NG + k + 1 + START)
                copy_group(nc.scalar.copy, j, k, t0, n).then_inc(copied, 1)

        with act.Fori(0, PARTS) as part:
            for j in range(RT):
                tile = part * RT + j
                if path.factored:
                    act.wait_ge(nat_ready, tile + 1)
                    nc.scalar.activation(gview(rows_of[j], j % 4), gview(rows_of[j], j % 4), ACT.Exp).then_inc(nat_exp, 1)
                if j == 0:
                    act.wait_ge(factored, part * (ng * D) + START)
                    act.wait_ge(biased, part * (nd * D) + START)
                if j:
                    copy_groups(part, j - 1)
            copy_groups(part, RT - 1)

            def take(pair, b):
                act.wait_ge(weighed, (part * D + pair * 2 + b + 1) * NT + CREDIT)
                act.wait_ge(out_stored[b], (part * HALF + pair) * (16 * CH) + START)
                nc.scalar.copy(attended[b][0:96 + VC, :], acc[0:96 + VC, b, 0:CHW]).then_inc(acc_free[b], 1)

            def batch(pair, b, previous):
                before = part * D + pair * 2 + b
                for n, unit in enumerate(path.exps):
                    if n == 7 and previous is not None:
                        take(*previous)
                    first, last = path.buffer(b, unit[0]), path.buffer(b, unit[-1])
                    if path.kind[unit[0]] == "d":
                        act.wait_ge(biased, before * nd + path.before(unit[-1], "d") + 1 + START)
                        e = xd[:, first:last + 1, :]
                        nc.scalar.activation(e, e, ACT.Exp).then_inc(exped, 1)
                    else:
                        t = unit[0]
                        act.wait_ge(scored, before * NT + t + 1 + CREDIT)
                        act.wait_ge(weighed, before * NT + path.weighed_since(b, t) + CREDIT)
                        nc.scalar.activation(xg[:, first, :], scores[:, path.slot(t), 0:W], ACT.Exp).then_inc(exped, 1)

            batch(0, 0, None)
            batch(0, 1, (0, 0))
            with act.Fori(1, HALF) as pair:
                batch(pair, 0, (pair - 1, 1))
                batch(pair, 1, (pair, 0))
            take(HALF - 1, 1)

    def gpsimd(pool):
        if not path.factored:
            return
        with pool.Fori(0, PARTS) as part:
            with pool.Fori(0, HALF) as pair:
                pool.wait_ge(copied, (part + 1) * (NG * RT) + NG)
                for b in range(2):
                    before = part * D + pair * 2 + b
                    for t in range(NT):
                        if path.kind[t] != "g":
                            continue
                        e = xg[:, path.buffer(b, t), :]
                        pool.wait_ge(exped, before * ne + path.exped_with(t))
                        nc.gpsimd.tensor_tensor(e[:, :], e[:, :], bias[:, t, :], ALU.mult).then_inc(factored, 1)

    run, trial = xd[:, 0, :], xd[:, 1, :]
    cmax = small[:, 8:8 + RT]
    cneg = small[0:RT, 32:32 + P]
    crest = small[0:RT, 160:160 + P]
    cpiece = small[0:RT, 288:288 + SPLIT * P // 2].bitcast(bf16).rearrange("r (s n) -> r s n", s=SPLIT)
    if not path.factored:
        m_loaded, m_scored, m_added, m_run = (sem(f"max_{s}") for s in ("loaded", "scored", "added", "run"))
        m_turned, m_column, m_row, m_chain = (sem(f"max_{s}") for s in ("turned", "column", "row", "chain"))
        m_ready, m_stored, m_zeroed = sem("max_ready"), sem("max_stored"), sem("max_zeroed")

    def find_maxima_sync(sp, part):
        with sp.Fori(0, D) as d:
            seen = part * D + d
            sp.wait_ge(scored, part * (D * NT) + CREDIT)
            sp.wait_ge(m_scored, seen * NT + START)
            load_batch(sp, d, part, 0, m_loaded, shifted=False)
            sp.wait_ge(m_ready, seen + 1)
            at = d * N + part * STEP
            sp.dma_start(shift_d[:, bass.ds(at, (RT - 1) * P)].rearrange("s (r n) -> r s n", n=P),
                         cpiece[0:RT - 1]).then_inc(m_stored, 16)
            sp.dma_start(shift_d[:, bass.ds(at + (RT - 1) * P, RLAST)].unsqueeze(0),
                         cpiece[RT - 1:RT, :, 0:RLAST]).then_inc(m_stored, 16)
        sp.wait_ge(m_stored, (part + 1) * (D * 32) + START)

    def find_maxima_tensor(pe, part):
        with pe.Fori(0, D) as d:
            seen = part * D + d
            pe.wait_ge(copied, (part + 1) * (NG * RT) + NG)
            pe.wait_ge(m_loaded, (seen + 1) * (16 * 2 * SPLIT))
            pe.wait_ge(m_zeroed, part + 1)
            for t in range(NT):
                pe.wait_ge(m_added, seen * NT + max(t - SLOTS + 1, 0) + START)
                for a, w in SEGS:
                    last = nc.tensor.matmul(scores[:, t % SLOTS, a:a + w], keys[0][:, t * P:(t + 1) * P],
                                            queries[0][:, a:a + w], start=True, stop=True)
                last.then_inc(m_scored, 1)
            pe.wait_ge(m_run, (seen + 1) * NT + START)
            for r in range(RT):
                w = rows_of[r]
                last = nc.tensor.transpose(banks[0:w, r // 4, P * (r % 4):P * (r % 4 + 1)], run[:, r * P:r * P + w],
                                           ident[:, :])
            last.then_inc(m_turned, 1)
            pe.wait_ge(m_column, seen + 1)
            nc.tensor.transpose(acc[0:RT, 0, 0:P], cmax, ident[:, :]).then_inc(m_row, 1)

    def find_maxima_vector(dve, part):
        LINKS = 5
        dve.wait_ge(scored, part * (D * NT) + CREDIT)
        nc.vector.memset(queries[0][0:SPLIT, :], 0.0).then_inc(m_zeroed, 1)
        with dve.Fori(0, D) as d:
            seen = part * D + d
            links = [0]
            dve.wait_ge(copied, (part + 1) * (NG * RT) + NG)
            dve.wait_ge(weighed, part * (D * NT) + CREDIT)
            dve.wait_ge(m_stored, seen * 32 + START)

            def link(ins):
                links[0] += 1
                ins.then_inc(m_chain, 1)
                dve.wait_ge(m_chain, seen * LINKS + links[0])

            link(nc.vector.memset(run[:, :], -3.0e38))
            for t in range(NT):
                dve.wait_ge(m_scored, seen * NT + t + 1 + START)
                dve.wait_ge(m_run, seen * NT + t + START)
                nc.vector.tensor_tensor(trial[:, :], scores[:, t % SLOTS, 0:W], bias[:, t, :], ALU.add).then_inc(m_added, 1)
                dve.wait_ge(m_added, seen * NT + t + 1 + START)
                nc.vector.tensor_tensor(run[:, :], run[:, :], trial[:, :], ALU.max).then_inc(m_run, 1)
            dve.wait_ge(m_turned, seen + 1)
            link(nc.vector.memset(cmax, 0.0))
            nc.vector.tensor_reduce(cmax[:, 0:RT - 1], flatp[:, 0:(RT - 1) * P].rearrange("p (r n) -> p r n", n=P), AX.X,
                                    ALU.max, negate=True)
            nc.vector.tensor_reduce(cmax[0:RLAST, RT - 1:RT], flatp[0:RLAST, (RT - 1) * P:RT * P], AX.X, ALU.max,
                                    negate=True).then_inc(m_column, 1)
            dve.wait_ge(m_row, seen + 1)
            link(nc.vector.tensor_copy(cpiece[:, 0, :], acc[0:RT, 0, 0:P]))
            link(nc.vector.tensor_tensor(crest, acc[0:RT, 0, 0:P], cpiece[:, 0, :], ALU.subtract))
            link(nc.vector.tensor_copy(cpiece[:, 1, :], crest))
            nc.vector.tensor_tensor(cpiece[:, 2, :], crest, cpiece[:, 1, :], ALU.subtract).then_inc(m_ready, 1)
            assert links[0] == LINKS

    return {"sync": sync, "tensor": tensor, "vector": vector, "scalar": scalar, "gpsimd": gpsimd}


def value_band(v_d, first):
    flat = v_d.rearrange("y c -> (y c)")[bass.ds(first, P * VROW)]
    return flat.rearrange("(y c) -> y c", c=VROW)[:, 0:NT * VC]


def project(nc, sem, carve, x, wo, o_d, out, ident, banks, flatp, acc):
    wo_raw = carve(H * P)
    wo_t = carve(H * P).rearrange("p (h o) -> p h o", o=P)
    heads = [carve(VC * P).rearrange("p (h g) -> p h g", g=P) for _ in range(4)]
    heads_t = [carve(H * P).rearrange("p (h r) -> p h r", r=P) for _ in range(2)]
    recip = [carve(P) for _ in range(4)]
    x_in = [carve(P) for _ in range(4)]
    y = [carve(P) for _ in range(4)]
    o_rows = o_d.rearrange("h (r g) -> r h g", g=P)

    wo_loaded, wo_turned, wo_ready = sem("wo_loaded"), sem("wo_turned"), sem("wo_ready")
    loaded = [sem(f"heads_loaded{b}") for b in range(4)]
    inverted, divided, turned, copied = sem("inverted"), sem("divided"), sem("heads_turned"), sem("heads_copied")
    summed, added = sem("summed"), sem("added")
    y_stored = [sem(f"y_stored{b}") for b in range(4)]
    FOUR, TWO = 4, 2
    QUADS = NT // 4
    rows_of = lambda i: P if i < NT - 1 else LAST

    with nc.Block() as block:
        def all_tiles(engine, tile):
            with engine.Fori(0, QUADS) as quad:
                for b in range(4):
                    tile(quad, b)
            for b in range(NT - 4 * QUADS):
                tile(QUADS, b)

        @block.sync
        def _(sp):
            for s, credit in ((turned, FOUR), (added, FOUR), (copied, TWO), (summed, TWO)):
                sp.sem_inc(s, credit)
            for s in y_stored:
                sp.sem_inc(s, START)
            sp.dma_start(wo_raw, wo[:, :]).then_inc(wo_loaded, 16)

            def load(quad, b, rows=P):
                i = quad * 4 + b
                sp.wait_ge(turned, i + 1)
                sp.wait_ge(added, i + 1)
                sp.dma_start(heads[b], o_rows[bass.ds(i * P, P), :, :]).then_inc(loaded[b], 16)
                sp.dma_start(x_in[b][0:rows, :], x[bass.ds(i * P, rows), :]).then_inc(loaded[b], 16)

            def store(quad, b, rows=P):
                i = quad * 4 + b
                sp.wait_ge(added, i + 1 + FOUR)
                sp.dma_start(out[bass.ds(i * P, rows), :], y[b][0:rows, :]).then_inc(y_stored[b], 16)

            for b in range(4):
                load(0, b)
            with sp.Fori(1, QUADS) as quad:
                for b in range(4):
                    load(quad, b)
                    store(quad - 1, b)
            for i in range(4 * QUADS, NT + 4):
                if i < NT:
                    load(i // 4, i % 4, rows_of(i))
                store(i // 4 - 1, i % 4, rows_of(i - 4))
            for b in range(4):
                sp.wait_ge(y_stored[b], 16 * len(range(b, NT, 4)) + START)

        @block.tensor
        def _(pe):
            pe.wait_ge(wo_loaded, 16)
            for h in range(H):
                last = nc.tensor.transpose(banks[:, h // 4, P * (h % 4):P * (h % 4 + 1)],
                                           wo_raw.rearrange("o (g h) -> o h g", h=H)[:, h, :], ident[:, :])
            last.then_inc(wo_turned, 1)
            pe.wait_ge(wo_ready, 1)

            def turn(i, b):
                pe.wait_ge(divided, i + 1)
                pe.wait_ge(copied, i + 1)
                for h in range(H):
                    last = nc.tensor.transpose(banks[:, 2 * (b % 2) + h // 4, P * (h % 4):P * (h % 4 + 1)],
                                               heads[b][:, h, :], ident[:, :])
                last.then_inc(turned, 1)

            def multiply(i, b):
                pe.wait_ge(copied, i + 1 + TWO)
                pe.wait_ge(added, i - 1 + FOUR)
                for h in range(H):
                    last = nc.tensor.matmul(acc[:, b % 2, 0:P], heads_t[b % 2][:, h, :], wo_t[:, h, :], start=(h == 0),
                                            stop=(h == H - 1))
                last.then_inc(summed, 1)

            def tile(quad, b):
                i = quad * 4 + b
                if not (quad is QUADS and i == NT - 1):
                    turn(i + 1, (b + 1) % 4)
                multiply(i, b)

            turn(0, 0)
            all_tiles(pe, tile)

        @block.scalar
        def _(act):
            act.wait_ge(wo_turned, 1)
            nc.scalar.copy(wo_t.rearrange("p h o -> p (h o)"), flatp[:, 0:H * P]).then_inc(wo_ready, 1)

            def tile(quad, b):
                i = quad * 4 + b
                act.wait_ge(turned, i + 1 + FOUR)
                act.wait_ge(summed, i + 1)
                nc.scalar.copy(heads_t[b % 2].rearrange("p h r -> p (h r)"),
                               flatp[:, 2 * (b % 2) * BANK:2 * (b % 2 + 1) * BANK]).then_inc(copied, 1)

            all_tiles(act, tile)

        @block.vector
        def _(dve):
            def divide(i, quad, b):
                dve.wait_ge(loaded[b], (quad + 1) * 32)
                nc.vector.reciprocal(recip[b], heads[b][:, H, :]).then_inc(inverted, 1)
                dve.wait_ge(inverted, i + 1)
                nc.vector.tensor_tensor(heads[b][:, 0:H, :], heads[b][:, 0:H, :],
                                        recip[b].unsqueeze(1).to_broadcast([P, H, P]), ALU.mult).then_inc(divided, 1)

            def add(i, quad, b):
                dve.wait_ge(summed, i + 1 + TWO)
                dve.wait_ge(y_stored[b], quad * 16 + START)
                nc.vector.tensor_tensor(y[b], acc[:, b % 2, 0:P], x_in[b], ALU.add).then_inc(added, 1)

            def tile(quad, b):
                i = quad * 4 + b
                if not (quad is QUADS and i + 2 >= NT):
                    divide(i + 2, quad + (b + 2) // 4, (b + 2) % 4)
                add(i, quad, b)

            for b in range(2):
                divide(b, 0, b)
            all_tiles(dve, tile)


_INS = ["x", "adj", "L0_gnn_Wq", "L0_gnn_Wk", "L0_gnn_Wv", "L0_gnn_Wo"]


def kernel(**inputs):
    import numpy as _np
    import concourse.bacc as _bacc
    from concourse import mybir as _mybir
    from concourse.bass_utils import run_bass_kernel_spmd as _run

    nc = _bacc.Bacc("TRN2", target_bir_lowering=False, num_devices=1)
    arrays, args = {}, []
    for name in _INS:
        a = _np.ascontiguousarray(inputs[name])
        arrays[f"in_{name}"] = a
        args.append(nc.dram_tensor(f"in_{name}", a.shape, _mybir.dt.from_np(a.dtype), kind="ExternalInput").ap())
    args.append(nc.dram_tensor("out", (N, D), fp32, kind="ExternalOutput").ap())
    build(nc, *args)
    r = _run(nc, [arrays], core_ids=[0])
    return r.results[0]["out"]
```

```python
from contextlib import ExitStack

import concourse.bass as bass
from concourse import mybir

N = 3327
D = 128
H = 8
P = 128
NT = (N + P - 1) // P
NPAD = NT * P
LAST = N - (NT - 1) * P
FLAT = NPAD * P
PARTS = 4
STEP = N // PARTS
W = N - (PARTS - 1) * STEP
RT = (W + P - 1) // P
RLAST = W - (RT - 1) * P
CH = 4
CHS = [W * c // CH for c in range(CH + 1)]
CHW = max(CHS[c + 1] - CHS[c] for c in range(CH))
VC = H + 1
SPLIT = 3
KR = SPLIT + SPLIT * SPLIT * H
SCALE = float(D) ** -0.5
EPS = 1e-5
MASKED = -1.0e30
SAFE = 34.0
BANK = 512
SLOTS = 3
START = 1
VROW = (NPAD + 1) * VC
RING = 3
XD, XG = 11, 3
ARENA = max(240 * P, (NT + XD + XG) * W)
GROUPS = [(4 * k, min(4, NT - 4 * k)) for k in range((NT + 3) // 4)]
SEGS = [(a, min(BANK, W - a)) for a in range(0, W, BANK)]

fp32 = mybir.dt.float32
bf16 = mybir.dt.bfloat16
i32 = mybir.dt.int32
ALU = mybir.AluOpType
ACT = mybir.ActivationFunctionType
AX = mybir.AxisListType


def build(nc, x, adj, wq, wk, wv, wo, out):
    qk_d = nc.dram_tensor("qk_pieces", [SPLIT, 2, H, FLAT], bf16).ap()
    shift_d = nc.dram_tensor("shift_pieces", [SPLIT, FLAT], bf16).ap()
    qnorm_d = nc.dram_tensor("qnorm", [FLAT], fp32).ap()
    v_d = nc.dram_tensor("values", [2 * P, VROW], fp32).ap()
    o_d = nc.dram_tensor("attended", [VC, FLAT], fp32).ap()

    ctx = ExitStack()
    with ctx:
        def sb(name, shape, dt=fp32):
            return ctx.enter_context(nc.sbuf_tensor(name, shape, dt))

        def sem(name):
            return ctx.enter_context(nc.semaphore(name))

        arena = sb("arena", [P, ARENA])
        bias = arena[:, 0:NT * W].rearrange("p (t n) -> p t n", n=W)
        used = [0]

        def carve(cols, dt=fp32):
            a = used[0]
            used[0] = a + cols
            v = arena[:, a:a + cols]
            return v if dt == fp32 else v.bitcast(dt)

        nat = [sb(f"nat{b}", [P, N]) for b in range(2)]
        keys = [sb(f"keys{b}", [KR, NPAD], bf16) for b in range(2)]
        queries = [sb(f"queries{b}", [KR, W], bf16) for b in range(2)]
        values = [sb(f"values{b}", [P, NT * VC]) for b in range(2)]
        xd = arena[:, NT * W:(NT + XD) * W].rearrange("p (b n) -> p b n", n=W)
        xg = arena[:, (NT + XD) * W:(NT + XD + XG) * W].rearrange("p (b n) -> p b n", n=W)
        assert 2 * N <= (XD + XG) * W
        nat_more = [arena[:, NT * W + b * N:NT * W + (b + 1) * N] for b in range(2)]
        attended = [sb(f"attended_sb{b}", [P, CHW]) for b in range(2)]
        ident = sb("ident", [P, P])
        small = sb("small", [P, 512])
        flag = sb("flag", [P, 1], i32)

        scores = ctx.enter_context(nc.psum_tensor("scores", [P, SLOTS, 2 * BANK], fp32))
        acc = ctx.enter_context(nc.psum_tensor("acc", [P, 2, BANK], fp32))
        banks = scores[:, :, :].rearrange("p a (b n) -> p (a b) n", n=BANK)
        flatp = scores[:, :, :].rearrange("p a n -> p (a n)")

        prepare(nc, sem, carve, x, wq, wk, wv, qk_d, qnorm_d, v_d, o_d, shift_d, nat, keys, ident, small, flag,
                banks, flatp, acc)
        attend(nc, sem, adj, qk_d, shift_d, v_d, o_d, bias, nat + nat_more, keys, queries, values, xd, xg, attended, ident,
               small, flag, scores, banks, flatp, acc)
        used[0] = 0
        project(nc, sem, carve, x, wo, o_d, out, ident, banks, flatp, acc)


def prepare(nc, sem, carve, x, wq, wk, wv, qk_d, qnorm_d, v_d, o_d, shift_d, nat, keys, ident, small, flag,
            banks, flatp, acc):
    x_all = carve(NT * P).rearrange("p (t c) -> p t c", c=P)
    sq_all = carve(NT * P).rearrange("p (t c) -> p t c", c=P)
    w_raw = [carve(H * P).rearrange("p (h c) -> p h c", c=P) for _ in range(3)]
    w_t = [carve(H * P).rearrange("p (h g) -> p h g", g=P) for _ in range(3)]
    h_row = [carve(P) for _ in range(2)]
    h_t = [carve(P) for _ in range(2)]
    pieces = [carve(SPLIT * 2 * H * 2 * P // 2, bf16).rearrange("p (s m h a g) -> p s m h a g", s=SPLIT, m=2, h=H, a=2)
              for _ in range(2)]
    v_room = [carve(2 * P * VC), sq_all.rearrange("p t c -> p (t c)")[:, 0:2 * P * VC]]
    v_out = [r.rearrange("p (r a h) -> p r a h", a=2, h=VC) for r in v_room]
    norm = [carve(4 * P).rearrange("p (m a g) -> p m a g", m=2, a=2) for _ in range(2)]
    rest = [nat[0][:, n * H * P:(n + 1) * H * P] for n in range(3)] + [nat[1][:, 0:H * P]]
    square = [nat[1][:, n * H * P:(n + 1) * H * P] for n in range(1, 3)]
    by_feature = lambda flat: flat.rearrange("p (h g) -> p h g", g=P)
    top = carve(2 * P).rearrange("p (m g) -> p m g", m=2)

    mean, var, root, inv = (small[:, 32 * i:32 * i + NT] for i in range(4))
    half = small[:, 128:128 + NT]
    peak, peaks, bound, keep, negkeep = (small[:, 160 + 2 * i:162 + 2 * i] for i in range(5))

    x_padded, x_loaded, w_loaded = sem("x_padded"), sem("x_loaded"), sem("w_loaded")
    filled, ident_ready, w_turned, w_ready = sem("filled"), sem("ident_ready"), sem("w_turned"), sem("w_ready")
    chain, var_ready, root_ready = sem("chain"), sem("var_ready"), sem("root_ready")
    h_ready, h_turned, h_t_ready = sem("h_ready"), sem("h_turned"), sem("h_t_ready")
    projected = [sem("q_projected"), sem("k_projected"), sem("v_projected")]
    first_piece = [sem("q_first"), sem("k_first")]
    squared = [sem("q_squared"), sem("k_squared")]
    rest_ready = [sem("q_rest"), sem("k_rest")]
    normed = [sem("q_normed"), sem("k_normed")]
    second_piece = [sem("q_second"), sem("k_second")]
    third_piece = [sem("q_third"), sem("k_third")]
    v_ready, norm_kept = sem("v_ready"), sem("norm_kept")
    stored = [sem("pieces_stored0"), sem("pieces_stored1")]
    v_stored = [sem("v_stored0"), sem("v_stored1")]
    peak_ready, peaks_ready = sem("peak_ready"), sem("peaks_ready")
    norms_loaded, clamped, shift_root = sem("norms_loaded"), sem("clamped"), sem("shift_root")
    shift_piece, shift_stored, pad_stored = sem("shift_piece"), sem("shift_stored"), sem("pad_stored")

    shift = nat[0]
    shift_rest = nat[1]

    qk_rows = qk_d.rearrange("s m h (r g) -> r (s m h) g", g=2 * P)
    norm_rows = qnorm_d.rearrange("(r g) -> r g", g=2 * P)
    piece_a, piece_b = (sq_all.rearrange("p t c -> p (t c)").bitcast(bf16)[:, n:n + N] for n in (0, NPAD))
    piece_c = x_all.rearrange("p t c -> p (t c)").bitcast(bf16)[:, 0:N]

    PAIRS = NT // 2

    def all_pairs(engine, work):
        with engine.Fori(0, PAIRS // 2) as two:
            for b in range(2):
                work(two * 2 + b, b, two)
        work(PAIRS - 1, 0, PAIRS // 2)

    with nc.Block() as block:
        @block.sync
        def _(sp):
            for s in (h_t_ready, h_turned, v_ready, projected[2], *squared, *rest_ready, *normed, *second_piece, *third_piece,
                      *stored, *v_stored):
                sp.sem_inc(s, START)
            x_pairs = x_all.rearrange("p (q a) c -> p q a c", a=2)
            sp.dma_start(x_pairs[:, 0:PAIRS - 1],
                         x[0:(NT - 2) * P, :].rearrange("(q p a) c -> p q a c", p=P, a=2)).then_inc(x_loaded, 16)
            sp.wait_ge(x_padded, 1)
            sp.dma_start(x_pairs[0:P - 1, PAIRS - 1],
                         x[(NT - 2) * P:N - 1, :].rearrange("(p a) c -> p a c", a=2)).then_inc(x_loaded, 16)
            sp.dma_start(x_pairs[P - 1:P, PAIRS - 1, 0], x[N - 1:N, :]).then_inc(x_loaded, 16)
            for m, w in enumerate((wq, wk, wv)):
                sp.dma_start(w_raw[m], w.rearrange("(g h) c -> g h c", h=H)).then_inc(w_loaded, 16)

            def store(pair, b, before):
                for m in range(2):
                    sp.wait_ge(second_piece[m], pair * 2 + 2 + START)
                    sp.wait_ge(third_piece[m], pair * 2 + 2 + START)
                sp.wait_ge(normed[0], pair * 2 + 2 + START)
                sp.dma_start(qk_rows[bass.ds(pair * P, P), :, :],
                             pieces[b].rearrange("p s m h a g -> p (s m h) (a g)")).then_inc(stored[b], 16)
                sp.dma_start(norm_rows[bass.ds(pair * P, P), :],
                             norm[b][:, 0, :, :].rearrange("p a g -> p (a g)")).then_inc(stored[b], 16)
                sp.wait_ge(v_ready, pair * 2 + 2 + START)
                sp.dma_start(v_d[P:2 * P, bass.ds(pair * (2 * P * VC), 2 * P * VC)], v_room[b]).then_inc(v_stored[b], 16)
                sp.dma_start(v_d[0:P, bass.ds(pair * (2 * P * VC) + VC, 2 * P * VC)], v_room[b]).then_inc(v_stored[b], 16)

            all_pairs(sp, store)
            sp.wait_ge(filled, 1)
            sp.dma_start(o_d[:, N * P:FLAT], small[0:VC, 256:256 + P]).then_inc(pad_stored, 16)
            for b in range(2):
                sp.wait_ge(stored[b], 32 * len(range(b, PAIRS, 2)) + START)
                sp.wait_ge(v_stored[b], 32 * len(range(b, PAIRS, 2)) + START)
            sp.dma_start(shift[:, :], qnorm_d[0:N * D].rearrange("(d n) -> d n", n=N)).then_inc(norms_loaded, 16)
            for s, piece in enumerate((piece_a, piece_b, piece_c)):
                sp.wait_ge(shift_piece, s + 1)
                sp.dma_start(shift_d[s, 0:N * D].rearrange("(d n) -> d n", n=N), piece).then_inc(shift_stored, 16)
            sp.dma_start(shift_d[:, N * D:FLAT], small[0:SPLIT, 384:384 + P // 2].bitcast(bf16)).then_inc(shift_stored, 16)
            sp.wait_ge(shift_stored, 64)
            sp.wait_ge(pad_stored, 16)

        @block.gpsimd
        def _(pool):
            nc.gpsimd.memset(small[:, 256:384], 1.0)
            nc.gpsimd.memset(small[:, 384:512], 0.0).then_inc(filled, 1)
            nc.gpsimd.memset(ident[:, :], 0.0).then_inc(ident_ready, 1)
            pool.wait_ge(ident_ready, 1)
            nc.gpsimd.affine_select(out=ident[:, :], in_=ident[:, :], compare_op=ALU.not_equal, fill=1.0, base=0,
                                    pattern=[[-1, P]], channel_multiplier=1).then_inc(ident_ready, 1)
            for b in range(2):
                nc.gpsimd.memset(keys[b][0:SPLIT, :], 1.0)

            def third(pair, b, before):
                for a in range(2):
                    i = pair * 2 + a
                    for m in range(2):
                        pool.wait_ge(second_piece[m], i + 1 + START)
                        nc.gpsimd.tensor_tensor(pieces[b][:, 2, m, :, a, :], by_feature(rest[2 * a + m]),
                                                pieces[b][:, 1, m, :, a, :], ALU.subtract).then_inc(third_piece[m], 1)

            all_pairs(pool, third)
            pool.wait_ge(peak_ready, 1)
            nc.gpsimd.partition_all_reduce(peaks, peak, P, bass.bass_isa.ReduceOp.max).then_inc(peaks_ready, 1)

        @block.tensor
        def _(pe):
            pe.wait_ge(ident_ready, 2)
            pe.wait_ge(w_loaded, 48)
            for m in range(3):
                for h in range(H):
                    last = nc.tensor.transpose(banks[:, 2 * m + h // 4, P * (h % 4):P * (h % 4 + 1)],
                                               w_raw[m][:, h, :], ident[:, :])
                last.then_inc(w_turned, 1)

            def turn(i, a):
                pe.wait_ge(h_ready, i + 1)
                pe.wait_ge(h_t_ready, i + START)
                nc.tensor.transpose(acc[:, 0, 0:P], h_row[a], ident[:, :]).then_inc(h_turned, 1)

            def multiply(pair, b, before):
                for a in range(2):
                    i = pair * 2 + a
                    pe.wait_ge(h_t_ready, i + 1 + START)
                    if not (pair is PAIRS - 1 and a == 1):
                        turn(i + 1, 1 - a)
                    for m in range(2):
                        pe.wait_ge(squared[m], i + START)
                        pe.wait_ge(rest_ready[m], i + START)
                        for s in range(2):
                            last = nc.tensor.matmul(banks[:, 2 * m + s, :], h_t[a],
                                                    w_t[m][:, 4 * s:4 * s + 4, :].rearrange("p h g -> p (h g)"),
                                                    start=True, stop=True)
                        last.then_inc(projected[m], 1)
                    pe.wait_ge(v_ready, i + START)
                    for h in range(H):
                        last = nc.tensor.matmul(banks[:, 4 + h // 4, P * (h % 4):P * (h % 4 + 1)], w_t[2][:, h, :],
                                                h_t[a], start=True, stop=True)
                    last.then_inc(projected[2], 1)

            turn(0, 0)
            pe.wait_ge(w_ready, 3)
            all_pairs(pe, multiply)

        @block.scalar
        def _(act):
            act.wait_ge(var_ready, 1)
            nc.scalar.activation(root, var, ACT.Sqrt).then_inc(root_ready, 1)
            for m in range(3):
                act.wait_ge(w_turned, m + 1)
                nc.scalar.copy(w_t[m].rearrange("p h g -> p (h g)"),
                               flatp[:, 2 * m * BANK:2 * (m + 1) * BANK]).then_inc(w_ready, 1)

            def copy_turned(i, a):
                act.wait_ge(h_turned, i + 1 + START)
                act.wait_ge(projected[2], i - 1 + START)
                nc.scalar.copy(h_t[a], acc[:, 0, 0:P]).then_inc(h_t_ready, 1)

            def split(pair, b, before):
                for a in range(2):
                    i = pair * 2 + a
                    if not (pair is PAIRS - 1 and a == 1):
                        copy_turned(i + 1, 1 - a)
                    act.wait_ge(stored[b], before * 32 + START)
                    for m in range(2):
                        src = flatp[:, 2 * m * BANK:2 * (m + 1) * BANK]
                        scale = SCALE if m == 0 else 1.0
                        act.wait_ge(projected[m], i + 1)
                        nc.scalar.activation(pieces[b][:, 0, m, :, a, :], by_feature(src), ACT.Copy,
                                             scale=scale).then_inc(first_piece[m], 1)
                        act.wait_ge(normed[m], i + START)
                        nc.scalar.activation(square[m], src, ACT.Square, scale=scale).then_inc(squared[m], 1)
                    for m in range(2):
                        act.wait_ge(rest_ready[m], i + 1 + START)
                        nc.scalar.copy(pieces[b][:, 1, m, :, a, :],
                                       by_feature(rest[2 * a + m])).then_inc(second_piece[m], 1)

            act.wait_ge(h_turned, 1 + START)
            nc.scalar.copy(h_t[0], acc[:, 0, 0:P]).then_inc(h_t_ready, 1)
            all_pairs(act, split)
            act.wait_ge(clamped, 1)
            nc.scalar.activation(shift[:, :], shift[:, :], ACT.Sqrt).then_inc(shift_root, 1)

        @block.vector
        def _(dve):
            links = [0]

            def link(ins):
                links[0] += 1
                ins.then_inc(chain, 1)
                dve.wait_ge(chain, links[0])

            nc.vector.memset(x_all[:, NT - 1, :], 0.0).then_inc(x_padded, 1)
            nc.vector.memset(top, 0.0)
            nc.vector.memset(v_room[0], 1.0)
            link(nc.vector.memset(acc[:, :, :], 0.0))
            dve.wait_ge(x_loaded, 48)
            link(nc.vector.reduce_sum(mean, x_all, axis=AX.X))
            link(nc.vector.tensor_scalar(mean, mean, 1.0 / D, None, ALU.mult))
            link(nc.vector.tensor_tensor(x_all, x_all, mean.unsqueeze(2).to_broadcast([P, NT, P]), ALU.subtract))
            link(nc.vector.tensor_tensor(sq_all, x_all, x_all, ALU.mult))
            link(nc.vector.reduce_sum(var, sq_all, axis=AX.X))
            nc.vector.tensor_scalar(var, var, 1.0 / D, EPS, ALU.mult, ALU.add).then_inc(var_ready, 1)
            dve.wait_ge(var_ready, 1)
            nc.vector.memset(v_room[1], 1.0)
            dve.wait_ge(root_ready, 1)
            link(nc.vector.reciprocal(inv, root))
            link(nc.vector.tensor_tensor(half, var, inv, ALU.mult))
            link(nc.vector.tensor_tensor(half, half, root, ALU.add))
            link(nc.vector.tensor_scalar(half, half, 0.5, None, ALU.mult))
            link(nc.vector.reciprocal(inv, half))
            link(nc.vector.tensor_tensor(x_all, x_all, inv.unsqueeze(2).to_broadcast([P, NT, P]), ALU.mult))

            def clip(i, a):
                tile = x_all[:, i, :] if isinstance(i, int) else x_all[:, bass.ds(i, 1), :].rearrange("p o c -> p (o c)")
                nc.vector.tensor_scalar(h_row[a], tile, 0.0, None, ALU.max).then_inc(h_ready, 1)

            def rests(pair, b, before):
                for a in range(2):
                    i = pair * 2 + a
                    if pair is not PAIRS - 1:
                        dve.wait_ge(h_turned, i + 1 + START)
                        clip(i + 2, a)
                    for m in range(2):
                        src = flatp[:, 2 * m * BANK:2 * (m + 1) * BANK]
                        dve.wait_ge(first_piece[m], i + 1)
                        dve.wait_ge(third_piece[m], pair * 2 + START)
                        dve.wait_ge(squared[m], i + 1 + START)
                        nc.vector.scalar_tensor_tensor(by_feature(rest[2 * a + m]), by_feature(src),
                                                       SCALE if m == 0 else 1.0, pieces[b][:, 0, m, :, a, :], ALU.mult,
                                                       ALU.subtract).then_inc(rest_ready[m], 1)
                        dve.wait_ge(stored[b], before * 32 + START)
                        nc.vector.reduce_sum(norm[b][:, m, a, :], square[m].rearrange("p (h g) -> p g h", g=P),
                                             axis=AX.X).then_inc(normed[m], 1)
                    dve.wait_ge(projected[2], i + 1 + START)
                    dve.wait_ge(v_stored[b], before * 32 + START)
                    nc.vector.tensor_copy(v_out[b][:, :, a, 0:H],
                                          flatp[:, 4 * BANK:6 * BANK].rearrange("p (h r) -> p r h", r=P)).then_inc(v_ready, 1)
                    dve.wait_ge(normed[1], i + 1 + START)
                    nc.vector.tensor_tensor(top, top, norm[b][:, :, a, :], ALU.max).then_inc(norm_kept, 1)
                    dve.wait_ge(norm_kept, i + 1)

            for a in range(2):
                clip(a, a)
            all_pairs(dve, rests)
            nc.vector.tensor_reduce(peak, top, AX.X, ALU.max).then_inc(peak_ready, 1)
            dve.wait_ge(peaks_ready, 1)
            link(nc.vector.tensor_tensor(bound[:, 0:1], peaks[:, 0:1], peaks[:, 1:2], ALU.mult))
            link(nc.vector.tensor_scalar(keep[:, 0:1], bound[:, 0:1], SAFE * SAFE, None, ALU.is_le))
            nc.vector.tensor_copy(flag[:, :], keep[:, 0:1])
            link(nc.vector.tensor_scalar(negkeep[:, 0:1], keep[:, 0:1], -1.0, None, ALU.mult))
            dve.wait_ge(norms_loaded, 16)
            nc.vector.tensor_scalar(shift[:, :], shift[:, :], peaks[:, 1:2], 1e-30, ALU.mult, ALU.max).then_inc(clamped, 1)
            dve.wait_ge(shift_root, 1)
            link(nc.vector.tensor_scalar(shift[:, :], shift[:, :], negkeep[:, 0:1], None, ALU.mult))
            nc.vector.tensor_copy(piece_a, shift[:, :]).then_inc(shift_piece, 1)
            dve.wait_ge(shift_piece, 1)
            link(nc.vector.tensor_tensor(shift_rest[:, :], shift[:, :], piece_a, ALU.subtract))
            nc.vector.tensor_copy(piece_b, shift_rest[:, :]).then_inc(shift_piece, 1)
            dve.wait_ge(shift_piece, 2)
            nc.vector.tensor_tensor(piece_c, shift_rest[:, :], piece_b, ALU.subtract).then_inc(shift_piece, 1)


class Path:

    def __init__(self, name, factored):
        self.name = name
        self.factored = factored
        self.kind = ["g" if factored and t % 4 == 3 else "d" for t in range(NT)]
        self.skip = NT - 1
        assert (NT + 1) % SLOTS == 0
        self.nd, self.ng = self.kind.count("d"), self.kind.count("g")
        self.order = sorted(range(NT), key=lambda t: t + (2 if self.kind[t] == "g" else 0))
        self.group, self.ring = (3, RING) if factored else (2, 2)
        direct = [t for t in range(NT) if self.kind[t] == "d"]
        self.full = self.nd // self.group
        self.ahead = 9 if factored else 4
        assert 2 * self.full % self.ring == 0
        self.groups = [tuple(direct[n:n + self.group]) for n in range(0, self.nd, self.group)]
        self.exps = sorted(self.groups + [(t,) for t in range(NT) if self.kind[t] == "g"],
                           key=lambda unit: unit[-1] - (1.5 if self.kind[unit[0]] == "g" else 0))
        self.ne = len(self.exps)

    def exped_with(self, t):
        return [t in unit for unit in self.exps].index(True) + 1

    def buffer(self, b, t):
        if self.kind[t] == "g":
            n, full = self.before(t, "g"), self.ng // RING * RING
            return (b * full + n) % RING if n < full else RING
        u = [t in group for group in self.groups].index(True)
        place = self.groups[u].index(t)
        return place + self.group * ((b * self.full + u) % self.ring if u < self.full else self.ring)

    def weighed_since(self, b, t):
        same = [u for u in range(NT) if self.kind[u] == self.kind[t]]
        for u in reversed([u for u in same if u < t]):
            if self.buffer(b, u) == self.buffer(b, t):
                return self.order.index(u) + 1
        for u in reversed(same):
            if self.buffer(1 - b, u) == self.buffer(b, t):
                return self.order.index(u) + 1 - NT

    def slot(self, t):
        return (t + (1 if t >= self.skip else 0)) % SLOTS

    def slot_holder(self, t):
        for ago, tiles in ((0, range(t)), (1, range(NT))):
            same = [u for u in tiles if self.slot(u) == self.slot(t)]
            if same:
                return same[-1], ago

    def before(self, t, kind):
        return self.kind[:t].count(kind)


def attend(nc, sem, adj, qk_d, shift_d, v_d, o_d, bias, nat, keys, queries, values, xd, xg, attended, ident, small,
           flag, scores, banks, flatp, acc):
    fast, general = Path("fast", True), Path("general", False)
    args = (adj, qk_d, shift_d, v_d, o_d, bias, nat, keys, queries, values, xd, xg, attended, ident, small, scores,
            banks, flatp, acc)
    programs = [attention_programs(nc, sem, path, *args) for path in (fast, general)]
    ready = sem("attention_constants")

    with nc.Block() as block:
        def either(engine, which):
            bounded = engine.value_load(flag[0:1, 0:1], min_val=0, max_val=1)
            with engine.If(bounded == 1):
                programs[0][which](engine)
            with engine.Else():
                programs[1][which](engine)

        @block.sync
        def _(sp):
            sp.wait_ge(ready, 1)
            either(sp, "sync")

        @block.gpsimd
        def _(pool):
            pool.wait_ge(ready, 1)
            either(pool, "gpsimd")

        @block.tensor
        def _(pe):
            pe.wait_ge(ready, 1)
            either(pe, "tensor")

        @block.scalar
        def _(act):
            act.wait_ge(ready, 1)
            either(act, "scalar")

        @block.vector
        def _(dve):
            nc.vector.memset(bias[96:P, NT - 1, :], MASKED)
            nc.vector.memset(acc[:, :, :], 0.0).then_inc(ready, 1)
            dve.wait_ge(ready, 1)
            either(dve, "vector")


def attention_programs(nc, sem, path, adj, qk_d, shift_d, v_d, o_d, bias, nat, keys, queries, values, xd, xg,
                       attended, ident, small, scores, banks, flatp, acc):
    name = path.name
    nd, ng, ne = path.nd, path.ng, path.ne

    nat_loaded = [sem(f"{name}_nat_loaded{b}") for b in range(4)]
    row_max, nat_ready, nat_exp = sem(f"{name}_row_max"), sem(f"{name}_nat_ready"), sem(f"{name}_nat_exp")
    turned, copied = sem(f"{name}_turned"), sem(f"{name}_copied")
    qk_loaded = [sem(f"{name}_qk_loaded{b}") for b in range(2)]
    v_loaded = [sem(f"{name}_v_loaded{b}") for b in range(2)]
    scored = sem(f"{name}_scored")
    biased = sem(f"{name}_biased")
    exped = sem(f"{name}_exped")
    factored = sem(f"{name}_factored")
    weighed = sem(f"{name}_weighed")
    acc_free = [sem(f"{name}_acc_free{b}") for b in range(2)]
    out_stored = [sem(f"{name}_out_stored{b}") for b in range(2)]
    CREDIT = NT + START
    HALF = D // 2

    gview = lambda rows, b: nat[b][0:rows, 0:24 * P].rearrange("p (a q c) -> p a q c", q=4, c=P)[:, :, 3, :]
    rows_of = [P] * (RT - 1) + [RLAST]
    loads_of = [len(range(b, RT, 4)) for b in range(4)]
    NG = len(GROUPS)

    def natural_count(part, j):
        return part * loads_of[j % 4] + j // 4 + 1

    def load_adjacency(sp, part, tiles):
        for j in tiles:
            if j in (2, 3):
                sp.wait_ge(weighed, part * (D * NT) + CREDIT)
            elif j >= 4:
                sp.wait_ge(turned, part * (RT * NG) + (j - 3) * NG + START)
            else:
                sp.wait_ge(turned, part * (RT * NG) + START)
            sp.dma_start(nat[j % 4][0:rows_of[j], :],
                         adj[bass.ds(part * STEP + j * P, rows_of[j]), :]).then_inc(nat_loaded[j % 4], 16)

    def load_batch(sp, d, part, b, loaded, shifted=True):
        for s in range(SPLIT):
            r = SPLIT + s * SPLIT * H
            sp.dma_start(keys[b][r:r + SPLIT * H, :], qk_d[:, 1, :, bass.ds(d * N, NPAD)]).then_inc(loaded, 16)
            sp.dma_start(queries[b][r:r + SPLIT * H, :],
                         qk_d[s, 0, :, bass.ds(d * N + part * STEP, W)].unsqueeze(0).to_broadcast([SPLIT, H, W])
                         ).then_inc(loaded, 16)
        if shifted:
            sp.dma_start(queries[b][0:SPLIT, :], shift_d[:, bass.ds(d * N + part * STEP, W)]).then_inc(loaded, 16)

    BATCH_DMAS = 2 * SPLIT + 1

    def sync(sp):
        for s, credit in ((scored, CREDIT), (weighed, CREDIT)):
            sp.sem_inc(s, credit)
        for s in (*acc_free, *out_stored, turned, biased, factored):
            sp.sem_inc(s, START)
        sp.sem_inc(copied, NG)
        if not path.factored:
            for s in (m_scored, m_added, m_run, m_stored):
                sp.sem_inc(s, START)

        def attend_part(part, last=False):

            def load(pair, b):
                d = pair * 2 + b
                done = (part * D + d) * NT
                sp.wait_ge(scored, done - NT + CREDIT)
                sp.wait_ge(weighed, done - NT + CREDIT)
                load_batch(sp, d, part, b, qk_loaded[b])
                first = P * VROW - d * (VROW - NT * VC)
                sp.dma_start(values[b][:, :], value_band(v_d, first)).then_inc(v_loaded[b], 16)

            def store(pair, b):
                d = pair * 2 + b
                sp.wait_ge(acc_free[b], part * HALF + pair + 2)
                for c in range(CH):
                    w = CHS[c + 1] - CHS[c]
                    sp.dma_start(o_d[:, bass.ds(d * N + part * STEP + CHS[c], w)],
                                 attended[b][32 * c:32 * c + VC, 0:w]).then_inc(out_stored[b], 16)

            load_adjacency(sp, part, range(2, 4))
            if not path.factored:
                load_adjacency(sp, part, range(4, RT))
                find_maxima_sync(sp, part)
            for b in range(2):
                load(0, b)
            if path.factored:
                load_adjacency(sp, part, range(4, RT))
            with sp.Fori(1, HALF) as pair:
                for b in range(2):
                    load(pair, b)
                    store(pair - 1, b)
            if not last:
                load_adjacency(sp, part + 1, range(2))
            for b in range(2):
                store(HALF - 1, b)

        load_adjacency(sp, 0, range(2))
        with sp.Fori(0, PARTS - 1) as part:
            attend_part(part)
        attend_part(PARTS - 1, last=True)
        for b in range(2):
            sp.wait_ge(out_stored[b], 16 * CH * HALF * PARTS + START)

    def tensor(pe):
        with pe.Fori(0, PARTS) as part:
            pe.wait_ge(biased, part * (nd * D) + START)
            for b in range(2):
                pe.wait_ge(acc_free[b], part * HALF + 1)
            for j in range(RT):
                rows = rows_of[j]
                tile = part * RT + j
                if path.factored:
                    pe.wait_ge(nat_exp, tile + 1)
                pe.wait_ge(nat_ready, tile + 1)
                for k, (t0, n) in enumerate(GROUPS):
                    pe.wait_ge(copied, tile * NG + k + 1)
                    for t in range(t0, t0 + n):
                        cols = min(P, N - t * P)
                        last = nc.tensor.transpose(group_bank(k)[0:cols, P * (t - t0):P * (t - t0) + rows],
                                                   nat[j % 4][0:rows, t * P:t * P + cols], ident[0:rows, 0:rows])
                    last.then_inc(turned, 1)
            if not path.factored:
                find_maxima_tensor(pe, part)
            pe.wait_ge(copied, (part + 1) * (NG * RT) + NG)

            def score(pair, b, t, first=False):
                before = (part * D + pair * 2 + b)
                if t == 0:
                    pe.wait_ge(qk_loaded[b], (part * HALF + pair + 1) * (16 * BATCH_DMAS))
                holder, batches = path.slot_holder(t)
                batches = before - batches
                if not (first and t < SLOTS):
                    if path.kind[holder] == "d":
                        pe.wait_ge(biased, batches * nd + path.before(holder, "d") + 1 + START)
                    else:
                        pe.wait_ge(exped, batches * ne + path.exped_with(holder))
                for a, w in SEGS:
                    last = nc.tensor.matmul(scores[:, path.slot(t), a:a + w], keys[b][:, t * P:(t + 1) * P],
                                            queries[b][:, a:a + w], start=True, stop=True)
                last.then_inc(scored, 1)

            def weigh(pair, b, k):
                before = (part * D + pair * 2 + b)
                t = path.order[k]
                if k == 0:
                    pe.wait_ge(v_loaded[b], (part * HALF + pair + 1) * 16)
                    pe.wait_ge(acc_free[b], part * HALF + pair + 1)
                if path.kind[t] == "d":
                    pe.wait_ge(exped, before * ne + path.exped_with(t))
                    e = xd[:, path.buffer(b, t), :]
                else:
                    pe.wait_ge(factored, before * ng + path.before(t, "g") + 1 + START)
                    e = xg[:, path.buffer(b, t), :]
                for c in range(CH):
                    w = CHS[c + 1] - CHS[c]
                    last = nc.tensor.matmul(acc[32 * c:32 * c + VC, b, 0:w], values[b][:, t * VC:(t + 1) * VC],
                                            e[:, CHS[c]:CHS[c + 1]], start=(k == 0), stop=(k == NT - 1),
                                            tile_position=(0, 32 * c))
                last.then_inc(weighed, 1)

            AHEAD = path.ahead
            steps = [(b, t) for b in range(2) for t in range(NT)]
            for t in range(AHEAD):
                score(0, 0, t, first=True)
            with pe.Fori(0, HALF - 1) as pair:
                for s in range(0, len(steps), 2):
                    for nxt in (s + AHEAD, s + AHEAD + 1):
                        if nxt < len(steps):
                            score(pair, *steps[nxt])
                        else:
                            score(pair + 1, *steps[nxt - len(steps)])
                    for b, k in steps[s:s + 2]:
                        weigh(pair, b, k)
            for s in range(0, len(steps), 2):
                for nxt in (s + AHEAD, s + AHEAD + 1):
                    if nxt < len(steps):
                        score(HALF - 1, *steps[nxt])
                for b, k in steps[s:s + 2]:
                    weigh(HALF - 1, b, k)

    def vector(dve):
        amax = small[:, 0:4]
        with dve.Fori(0, PARTS) as part:
            for j in range(RT):
                rows = rows_of[j]
                tile = part * RT + j
                most = amax[0:rows, j % 4:j % 4 + 1]
                dve.wait_ge(nat_loaded[j % 4], natural_count(part, j) * 16)
                nc.vector.reduce_max(most, nat[j % 4][0:rows, :], AX.X).then_inc(row_max, 1)
                dve.wait_ge(row_max, tile + 1)
                nc.vector.tensor_scalar(nat[j % 4][0:rows, :], nat[j % 4][0:rows, :], most, 2.0,
                                        ALU.subtract, ALU.mult).then_inc(nat_ready, 1)
            if not path.factored:
                find_maxima_vector(dve, part)
            with dve.Fori(0, HALF) as pair:
                dve.wait_ge(copied, (part + 1) * (NG * RT) + NG)
                for b in range(2):
                    before = part * D + pair * 2 + b
                    for t in range(NT):
                        if path.kind[t] != "d":
                            continue
                        dve.wait_ge(scored, before * NT + t + 1 + CREDIT)
                        dve.wait_ge(weighed, before * NT + path.weighed_since(b, t) + CREDIT)
                        nc.vector.tensor_tensor(xd[:, path.buffer(b, t), :], scores[:, path.slot(t), 0:W], bias[:, t, :],
                                                ALU.add).then_inc(biased, 1)

    def group_bank(k):
        return banks[:, k, :] if k < 6 else acc[:, k - 6, :]

    def copy_group(copy, j, k, t0, n):
        rows = rows_of[j]
        bank = group_bank(k).rearrange("p (t c) -> p t c", c=P)
        if t0 + n < NT:
            return copy(bias[:, t0:t0 + n, j * P:j * P + rows], bank[:, 0:n, 0:rows])
        copy(bias[:, t0:t0 + n - 1, j * P:j * P + rows], bank[:, 0:n - 1, 0:rows])
        return copy(bias[0:LAST, NT - 1, j * P:j * P + rows], bank[0:LAST, n - 1, 0:rows])

    def scalar(act):
        def copy_groups(part, j):
            for k, (t0, n) in enumerate(GROUPS):
                act.wait_ge(turned, (part * RT + j) * NG + k + 1 + START)
                copy_group(nc.scalar.copy, j, k, t0, n).then_inc(copied, 1)

        with act.Fori(0, PARTS) as part:
            for j in range(RT):
                tile = part * RT + j
                if path.factored:
                    act.wait_ge(nat_ready, tile + 1)
                    nc.scalar.activation(gview(rows_of[j], j % 4), gview(rows_of[j], j % 4), ACT.Exp).then_inc(nat_exp, 1)
                if j == 0:
                    act.wait_ge(factored, part * (ng * D) + START)
                    act.wait_ge(biased, part * (nd * D) + START)
                if j:
                    copy_groups(part, j - 1)
            copy_groups(part, RT - 1)

            def take(pair, b):
                act.wait_ge(weighed, (part * D + pair * 2 + b + 1) * NT + CREDIT)
                act.wait_ge(out_stored[b], (part * HALF + pair) * (16 * CH) + START)
                nc.scalar.copy(attended[b][0:96 + VC, :], acc[0:96 + VC, b, 0:CHW]).then_inc(acc_free[b], 1)

            def batch(pair, b, previous):
                before = part * D + pair * 2 + b
                for n, unit in enumerate(path.exps):
                    if n == 7 and previous is not None:
                        take(*previous)
                    first, last = path.buffer(b, unit[0]), path.buffer(b, unit[-1])
                    if path.kind[unit[0]] == "d":
                        act.wait_ge(biased, before * nd + path.before(unit[-1], "d") + 1 + START)
                        e = xd[:, first:last + 1, :]
                        nc.scalar.activation(e, e, ACT.Exp).then_inc(exped, 1)
                    else:
                        t = unit[0]
                        act.wait_ge(scored, before * NT + t + 1 + CREDIT)
                        act.wait_ge(weighed, before * NT + path.weighed_since(b, t) + CREDIT)
                        nc.scalar.activation(xg[:, first, :], scores[:, path.slot(t), 0:W], ACT.Exp).then_inc(exped, 1)

            batch(0, 0, None)
            batch(0, 1, (0, 0))
            with act.Fori(1, HALF) as pair:
                batch(pair, 0, (pair - 1, 1))
                batch(pair, 1, (pair, 0))
            take(HALF - 1, 1)

    def gpsimd(pool):
        if not path.factored:
            return
        with pool.Fori(0, PARTS) as part:
            with pool.Fori(0, HALF) as pair:
                pool.wait_ge(copied, (part + 1) * (NG * RT) + NG)
                for b in range(2):
                    before = part * D + pair * 2 + b
                    for t in range(NT):
                        if path.kind[t] != "g":
                            continue
                        e = xg[:, path.buffer(b, t), :]
                        pool.wait_ge(exped, before * ne + path.exped_with(t))
                        nc.gpsimd.tensor_tensor(e[:, :], e[:, :], bias[:, t, :], ALU.mult).then_inc(factored, 1)

    run, trial = xd[:, 0, :], xd[:, 1, :]
    cmax = small[:, 8:8 + RT]
    crest = small[0:RT, 160:160 + P]
    cpiece = small[0:RT, 288:288 + SPLIT * P // 2].bitcast(bf16).rearrange("r (s n) -> r s n", s=SPLIT)
    if not path.factored:
        m_loaded, m_scored, m_added, m_run = (sem(f"max_{s}") for s in ("loaded", "scored", "added", "run"))
        m_turned, m_column, m_row, m_chain = (sem(f"max_{s}") for s in ("turned", "column", "row", "chain"))
        m_ready, m_stored, m_zeroed = sem("max_ready"), sem("max_stored"), sem("max_zeroed")

    def find_maxima_sync(sp, part):
        with sp.Fori(0, D) as d:
            seen = part * D + d
            sp.wait_ge(scored, part * (D * NT) + CREDIT)
            sp.wait_ge(m_scored, seen * NT + START)
            load_batch(sp, d, part, 0, m_loaded, shifted=False)
            sp.wait_ge(m_ready, seen + 1)
            at = d * N + part * STEP
            sp.dma_start(shift_d[:, bass.ds(at, (RT - 1) * P)].rearrange("s (r n) -> r s n", n=P),
                         cpiece[0:RT - 1]).then_inc(m_stored, 16)
            sp.dma_start(shift_d[:, bass.ds(at + (RT - 1) * P, RLAST)].unsqueeze(0),
                         cpiece[RT - 1:RT, :, 0:RLAST]).then_inc(m_stored, 16)
        sp.wait_ge(m_stored, (part + 1) * (D * 32) + START)

    def find_maxima_tensor(pe, part):
        with pe.Fori(0, D) as d:
            seen = part * D + d
            pe.wait_ge(copied, (part + 1) * (NG * RT) + NG)
            pe.wait_ge(m_loaded, (seen + 1) * (16 * 2 * SPLIT))
            pe.wait_ge(m_zeroed, part + 1)
            for t in range(NT):
                pe.wait_ge(m_added, seen * NT + max(t - SLOTS + 1, 0) + START)
                for a, w in SEGS:
                    last = nc.tensor.matmul(scores[:, t % SLOTS, a:a + w], keys[0][:, t * P:(t + 1) * P],
                                            queries[0][:, a:a + w], start=True, stop=True)
                last.then_inc(m_scored, 1)
            pe.wait_ge(m_run, (seen + 1) * NT + START)
            for r in range(RT):
                w = rows_of[r]
                last = nc.tensor.transpose(banks[0:w, r // 4, P * (r % 4):P * (r % 4 + 1)], run[:, r * P:r * P + w],
                                           ident[:, :])
            last.then_inc(m_turned, 1)
            pe.wait_ge(m_column, seen + 1)
            nc.tensor.transpose(acc[0:RT, 0, 0:P], cmax, ident[:, :]).then_inc(m_row, 1)

    def find_maxima_vector(dve, part):
        LINKS = 5
        dve.wait_ge(scored, part * (D * NT) + CREDIT)
        nc.vector.memset(queries[0][0:SPLIT, :], 0.0).then_inc(m_zeroed, 1)
        with dve.Fori(0, D) as d:
            seen = part * D + d
            links = [0]
            dve.wait_ge(copied, (part + 1) * (NG * RT) + NG)
            dve.wait_ge(weighed, part * (D * NT) + CREDIT)
            dve.wait_ge(m_stored, seen * 32 + START)

            def link(ins):
                links[0] += 1
                ins.then_inc(m_chain, 1)
                dve.wait_ge(m_chain, seen * LINKS + links[0])

            link(nc.vector.memset(run[:, :], -3.0e38))
            for t in range(NT):
                dve.wait_ge(m_scored, seen * NT + t + 1 + START)
                dve.wait_ge(m_run, seen * NT + t + START)
                nc.vector.tensor_tensor(trial[:, :], scores[:, t % SLOTS, 0:W], bias[:, t, :], ALU.add).then_inc(m_added, 1)
                dve.wait_ge(m_added, seen * NT + t + 1 + START)
                nc.vector.tensor_tensor(run[:, :], run[:, :], trial[:, :], ALU.max).then_inc(m_run, 1)
            dve.wait_ge(m_turned, seen + 1)
            link(nc.vector.memset(cmax, 0.0))
            nc.vector.tensor_reduce(cmax[:, 0:RT - 1], flatp[:, 0:(RT - 1) * P].rearrange("p (r n) -> p r n", n=P), AX.X,
                                    ALU.max, negate=True)
            nc.vector.tensor_reduce(cmax[0:RLAST, RT - 1:RT], flatp[0:RLAST, (RT - 1) * P:RT * P], AX.X, ALU.max,
                                    negate=True).then_inc(m_column, 1)
            dve.wait_ge(m_row, seen + 1)
            link(nc.vector.tensor_copy(cpiece[:, 0, :], acc[0:RT, 0, 0:P]))
            link(nc.vector.tensor_tensor(crest, acc[0:RT, 0, 0:P], cpiece[:, 0, :], ALU.subtract))
            link(nc.vector.tensor_copy(cpiece[:, 1, :], crest))
            nc.vector.tensor_tensor(cpiece[:, 2, :], crest, cpiece[:, 1, :], ALU.subtract).then_inc(m_ready, 1)
            assert links[0] == LINKS

    return {"sync": sync, "tensor": tensor, "vector": vector, "scalar": scalar, "gpsimd": gpsimd}


def value_band(v_d, first):
    flat = v_d.rearrange("y c -> (y c)")[bass.ds(first, P * VROW)]
    return flat.rearrange("(y c) -> y c", c=VROW)[:, 0:NT * VC]


def project(nc, sem, carve, x, wo, o_d, out, ident, banks, flatp, acc):
    wo_raw = carve(H * P)
    wo_t = carve(H * P).rearrange("p (h o) -> p h o", o=P)
    heads = [carve(VC * P).rearrange("p (h g) -> p h g", g=P) for _ in range(4)]
    heads_t = [carve(H * P).rearrange("p (h r) -> p h r", r=P) for _ in range(2)]
    recip = [carve(P) for _ in range(4)]
    x_in = [carve(P) for _ in range(4)]
    y = [carve(P) for _ in range(4)]
    o_rows = o_d.rearrange("h (r g) -> r h g", g=P)

    wo_loaded, wo_turned, wo_ready = sem("wo_loaded"), sem("wo_turned"), sem("wo_ready")
    loaded = [sem(f"heads_loaded{b}") for b in range(4)]
    inverted, divided, turned, copied = sem("inverted"), sem("divided"), sem("heads_turned"), sem("heads_copied")
    summed, added = sem("summed"), sem("added")
    y_stored = [sem(f"y_stored{b}") for b in range(4)]
    FOUR, TWO = 4, 2
    QUADS = NT // 4
    rows_of = lambda i: P if i < NT - 1 else LAST

    with nc.Block() as block:
        def all_tiles(engine, tile):
            with engine.Fori(0, QUADS) as quad:
                for b in range(4):
                    tile(quad, b)
            for b in range(NT - 4 * QUADS):
                tile(QUADS, b)

        @block.sync
        def _(sp):
            for s, credit in ((turned, FOUR), (added, FOUR), (copied, TWO), (summed, TWO)):
                sp.sem_inc(s, credit)
            for s in y_stored:
                sp.sem_inc(s, START)
            sp.dma_start(wo_raw, wo[:, :]).then_inc(wo_loaded, 16)

            def load(quad, b, rows=P):
                i = quad * 4 + b
                sp.wait_ge(turned, i + 1)
                sp.wait_ge(added, i + 1)
                sp.dma_start(heads[b], o_rows[bass.ds(i * P, P), :, :]).then_inc(loaded[b], 16)
                sp.dma_start(x_in[b][0:rows, :], x[bass.ds(i * P, rows), :]).then_inc(loaded[b], 16)

            def store(quad, b, rows=P):
                i = quad * 4 + b
                sp.wait_ge(added, i + 1 + FOUR)
                sp.dma_start(out[bass.ds(i * P, rows), :], y[b][0:rows, :]).then_inc(y_stored[b], 16)

            for b in range(4):
                load(0, b)
            with sp.Fori(1, QUADS) as quad:
                for b in range(4):
                    load(quad, b)
                    store(quad - 1, b)
            for i in range(4 * QUADS, NT + 4):
                if i < NT:
                    load(i // 4, i % 4, rows_of(i))
                store(i // 4 - 1, i % 4, rows_of(i - 4))
            for b in range(4):
                sp.wait_ge(y_stored[b], 16 * len(range(b, NT, 4)) + START)

        @block.tensor
        def _(pe):
            pe.wait_ge(wo_loaded, 16)
            for h in range(H):
                last = nc.tensor.transpose(banks[:, h // 4, P * (h % 4):P * (h % 4 + 1)],
                                           wo_raw.rearrange("o (g h) -> o h g", h=H)[:, h, :], ident[:, :])
            last.then_inc(wo_turned, 1)
            pe.wait_ge(wo_ready, 1)

            def turn(i, b):
                pe.wait_ge(divided, i + 1)
                pe.wait_ge(copied, i + 1)
                for h in range(H):
                    last = nc.tensor.transpose(banks[:, 2 * (b % 2) + h // 4, P * (h % 4):P * (h % 4 + 1)],
                                               heads[b][:, h, :], ident[:, :])
                last.then_inc(turned, 1)

            def multiply(i, b):
                pe.wait_ge(copied, i + 1 + TWO)
                pe.wait_ge(added, i - 1 + FOUR)
                for h in range(H):
                    last = nc.tensor.matmul(acc[:, b % 2, 0:P], heads_t[b % 2][:, h, :], wo_t[:, h, :], start=(h == 0),
                                            stop=(h == H - 1))
                last.then_inc(summed, 1)

            def tile(quad, b):
                i = quad * 4 + b
                if not (quad is QUADS and i == NT - 1):
                    turn(i + 1, (b + 1) % 4)
                multiply(i, b)

            turn(0, 0)
            all_tiles(pe, tile)

        @block.scalar
        def _(act):
            act.wait_ge(wo_turned, 1)
            nc.scalar.copy(wo_t.rearrange("p h o -> p (h o)"), flatp[:, 0:H * P]).then_inc(wo_ready, 1)

            def tile(quad, b):
                i = quad * 4 + b
                act.wait_ge(turned, i + 1 + FOUR)
                act.wait_ge(summed, i + 1)
                nc.scalar.copy(heads_t[b % 2].rearrange("p h r -> p (h r)"),
                               flatp[:, 2 * (b % 2) * BANK:2 * (b % 2 + 1) * BANK]).then_inc(copied, 1)

            all_tiles(act, tile)

        @block.vector
        def _(dve):
            def divide(i, quad, b):
                dve.wait_ge(loaded[b], (quad + 1) * 32)
                nc.vector.reciprocal(recip[b], heads[b][:, H, :]).then_inc(inverted, 1)
                dve.wait_ge(inverted, i + 1)
                nc.vector.tensor_tensor(heads[b][:, 0:H, :], heads[b][:, 0:H, :],
                                        recip[b].unsqueeze(1).to_broadcast([P, H, P]), ALU.mult).then_inc(divided, 1)

            def add(i, quad, b):
                dve.wait_ge(summed, i + 1 + TWO)
                dve.wait_ge(y_stored[b], quad * 16 + START)
                nc.vector.tensor_tensor(y[b], acc[:, b % 2, 0:P], x_in[b], ALU.add).then_inc(added, 1)

            def tile(quad, b):
                i = quad * 4 + b
                if not (quad is QUADS and i + 2 >= NT):
                    divide(i + 2, quad + (b + 2) // 4, (b + 2) % 4)
                add(i, quad, b)

            for b in range(2):
                divide(b, 0, b)
            all_tiles(dve, tile)


_INS = ["x", "adj", "L0_gnn_Wq", "L0_gnn_Wk", "L0_gnn_Wv", "L0_gnn_Wo"]


def kernel(**inputs):
    import numpy as _np
    import concourse.bacc as _bacc
    from concourse import mybir as _mybir
    from concourse.bass_utils import run_bass_kernel_spmd as _run

    nc = _bacc.Bacc("TRN2", target_bir_lowering=False, num_devices=1)
    arrays, args = {}, []
    for name in _INS:
        a = _np.ascontiguousarray(inputs[name])
        arrays[f"in_{name}"] = a
        args.append(nc.dram_tensor(f"in_{name}", a.shape, _mybir.dt.from_np(a.dtype), kind="ExternalInput").ap())
    args.append(nc.dram_tensor("out", (N, D), fp32, kind="ExternalOutput").ap())
    build(nc, *args)
    r = _run(nc, [arrays], core_ids=[0])
    return r.results[0]["out"]
```
